# Optimizing a Trainium2 kernel written in Bass

```python
import numpy as np
import jax
import jax.numpy as jnp

def _softmax(x, axis=-1):
    return jax.nn.softmax(x, axis=axis)

def _gelu(x):
    return jax.nn.gelu(x, approximate=True)

def _silu(x):
    return jax.nn.silu(x)

def _sigmoid(x):
    return jax.nn.sigmoid(x)

def _layernorm(x, axis=-1, eps=1e-05):
    m = jnp.mean(x, axis=axis, keepdims=True)
    v = jnp.var(x, axis=axis, keepdims=True)
    return (x - m) / jnp.sqrt(v + eps)

def _scatter_add(tgt, idx, src, axis=0):
    return tgt.at[idx].add(src)

def _segment_sum(src, seg, n):
    return jax.ops.segment_sum(src, seg, n)
kernel_name = 'mk_xattn_seq_d2_seqx_r4_2d4f19'

def setup_inputs(seed: int=0):
    np.random.seed(seed)
    _w = jnp.asarray

    def _rec_inputs():
        import jax
        import jax.numpy as jnp
        _rk = jax.random.key(seed)
        x = 7.22e-05 + 1 * jax.random.normal(jax.random.fold_in(_rk, 1), (16, 100, 512), jnp.float32)
        _lenS = 100 - jax.random.randint(jax.random.fold_in(_rk, 7), (16,), 0, max(1, 100 // 4) + 1, jnp.int32)
        _lenS2 = 361 - jax.random.randint(jax.random.fold_in(_rk, 8), (16,), 0, max(1, 361 // 4) + 1, jnp.int32)
        _ctx_2048P = jax.random.normal(jax.random.fold_in(_rk, 11), (16, 16, 512), jnp.float32)
        _ctx_2048c = jax.random.dirichlet(jax.random.fold_in(_rk, 511), 0.3 * jnp.ones((16,), jnp.float32), (16, 361))
        _ctx_2048t = jnp.einsum('bsk,bkd->bsd', _ctx_2048c, _ctx_2048P)
        _ctx_2048t = _ctx_2048t * jax.lax.rsqrt(jnp.mean(jnp.square(_ctx_2048t)) + 1e-12) * 0.953939
        ctx_2048 = 4.13588e-05 + 0.999923 * (_ctx_2048t + 0.3 * jax.random.normal(jax.random.fold_in(_rk, 611), (16, 361, 512), jnp.float32))
        _validS = jnp.arange(100)[None, :] < _lenS[:, None]
        _validS2 = jnp.arange(361)[None, :] < _lenS2[:, None]
        _causal = jnp.tril(jnp.ones((100, 100), dtype=bool))
        mask_Bx1xSxS2_ff0 = jnp.where(jnp.ones((16, 1, 100, 361), dtype=bool), 0.0, -1000000000.0).astype(jnp.float32)
        mask_BxS2_bf1 = jnp.ones((16, 361), dtype=bool)
        return (x, ctx_2048, mask_Bx1xSxS2_ff0, mask_BxS2_bf1)
    x, ctx_2048, mask_Bx1xSxS2_ff0, mask_BxS2_bf1 = _rec_inputs()

    def _L0_xattn_setup():
        import jax, jax.numpy as jnp
        import numpy as np
        H = 512
        NH = 32
        KVH = 8
        HD = H // NH
        GROUPS = NH // KVH
        EPS = 1e-06
        B, L, S = (4, 256, 256)

        def _gqa_forward(hidden_state, encoder_hidden_state, encoder_attention_mask, Wq, bq, Wk, bk, Wv, bv, Wo, bo, gamma, beta):
            b, l, _ = hidden_state.shape
            s = encoder_hidden_state.shape[1]
            q = hidden_state @ Wq + bq
            k = encoder_hidden_state @ Wk + bk
            v = encoder_hidden_state @ Wv + bv
            q = q.reshape(b, l, KVH, GROUPS, HD).transpose(0, 2, 3, 1, 4)
            k = k.reshape(b, s, KVH, HD).transpose(0, 2, 1, 3)
            v = v.reshape(b, s, KVH, HD).transpose(0, 2, 1, 3)
            scale = 1.0 / jnp.sqrt(jnp.asarray(HD, q.dtype))
            scores = jnp.einsum('bkgld,bksd->bkgls', q, k) * scale
            scores = scores + encoder_attention_mask[:, :, None, :, :]
            attn = jax.nn.softmax(scores, axis=-1)
            out = jnp.einsum('bkgls,bksd->bkgld', attn, v)
            out = out.transpose(0, 3, 1, 2, 4).reshape(b, l, H)
            out = out @ Wo + bo
            x = out + hidden_state
            mu = jnp.mean(x, axis=-1, keepdims=True)
            var = jnp.var(x, axis=-1, keepdims=True)
            return (x - mu) * jax.lax.rsqrt(var + EPS) * gamma + beta
        key = jax.random.key(seed)
        ks = jax.random.split(key, 12)
        sd = 0.02
        return {'hidden_state': jax.random.normal(ks[0], (B, L, H), jnp.float32), 'encoder_hidden_state': jax.random.normal(ks[1], (B, S, H), jnp.float32), 'encoder_attention_mask': jnp.zeros((B, 1, L, S), jnp.float32), 'Wq': jax.random.normal(ks[2], (H, H), jnp.float32) * sd, 'bq': jnp.zeros((H,), jnp.float32), 'Wk': jax.random.normal(ks[3], (H, KVH * HD), jnp.float32) * sd, 'bk': jnp.zeros((KVH * HD,), jnp.float32), 'Wv': jax.random.normal(ks[4], (H, KVH * HD), jnp.float32) * sd, 'bv': jnp.zeros((KVH * HD,), jnp.float32), 'Wo': jax.random.normal(ks[5], (H, H), jnp.float32) * sd, 'bo': jnp.zeros((H,), jnp.float32), 'gamma': jnp.ones((H,), jnp.float32), 'beta': jnp.zeros((H,), jnp.float32)}
    _L0_xattn_all = _L0_xattn_setup()
    _L0_xattn_in = {k: v for k, v in _L0_xattn_all.items() if k in ('Wq', 'bq', 'Wk', 'bk', 'Wv', 'bv', 'Wo', 'bo', 'gamma', 'beta')}
    del _L0_xattn_all

    def _L1_xattn_setup():
        import jax, jax.numpy as jnp
        import numpy as np
        HIDDEN = 512
        HEADS = 16
        HEAD_DIM = HIDDEN // HEADS
        LN_EPS = 1e-05
        GATE_INIT = 0.5

        def _layer_norm(x, gamma, beta):
            mu = jnp.mean(x, axis=-1, keepdims=True)
            var = jnp.mean(jnp.square(x - mu), axis=-1, keepdims=True)
            return (x - mu) * jax.lax.rsqrt(var + LN_EPS) * gamma + beta
        key = jax.random.key(seed)
        ks = jax.random.split(key, 8)
        B, T_TEXT, T_AUDIO = (4, 512, 375)
        s = 0.02
        return {'hidden_states': jax.random.normal(ks[0], (B, T_TEXT, HIDDEN), jnp.float32), 'audio_kv': jax.random.normal(ks[1], (B, T_AUDIO, HIDDEN), jnp.float32), 'audio_attention_mask': jnp.ones((B, T_AUDIO), dtype=bool), 'Wq': jax.random.normal(ks[2], (HIDDEN, HIDDEN), jnp.float32) * s, 'Wk': jax.random.normal(ks[3], (HIDDEN, HIDDEN), jnp.float32) * s, 'Wv': jax.random.normal(ks[4], (HIDDEN, HIDDEN), jnp.float32) * s, 'Wo': jax.random.normal(ks[5], (HIDDEN, HIDDEN), jnp.float32) * s, 'ln_gamma': jnp.ones((HIDDEN,), jnp.float32), 'ln_beta': jnp.zeros((HIDDEN,), jnp.float32), 'gate': jnp.array([GATE_INIT], jnp.float32)}
    _L1_xattn_all = _L1_xattn_setup()
    _L1_xattn_in = {k: v for k, v in _L1_xattn_all.items() if k in ('Wq', 'Wk', 'Wv', 'Wo', 'ln_gamma', 'ln_beta', 'gate')}
    del _L1_xattn_all
    return {'x': x, 'ctx_2048': ctx_2048, 'mask_Bx1xSxS2_ff0': mask_Bx1xSxS2_ff0, 'mask_BxS2_bf1': mask_BxS2_bf1, 'L0_xattn_Wq': _L0_xattn_in['Wq'], 'L0_xattn_bq': _L0_xattn_in['bq'], 'L0_xattn_Wk': _L0_xattn_in['Wk'], 'L0_xattn_bk': _L0_xattn_in['bk'], 'L0_xattn_Wv': _L0_xattn_in['Wv'], 'L0_xattn_bv': _L0_xattn_in['bv'], 'L0_xattn_Wo': _L0_xattn_in['Wo'], 'L0_xattn_bo': _L0_xattn_in['bo'], 'L0_xattn_gamma': _L0_xattn_in['gamma'], 'L0_xattn_beta': _L0_xattn_in['beta'], 'L1_xattn_Wq': _L1_xattn_in['Wq'], 'L1_xattn_Wk': _L1_xattn_in['Wk'], 'L1_xattn_Wv': _L1_xattn_in['Wv'], 'L1_xattn_Wo': _L1_xattn_in['Wo'], 'L1_xattn_ln_gamma': _L1_xattn_in['ln_gamma'], 'L1_xattn_ln_beta': _L1_xattn_in['ln_beta'], 'L1_xattn_gate': _L1_xattn_in['gate']}

def reference(x, ctx_2048, mask_Bx1xSxS2_ff0, mask_BxS2_bf1, L0_xattn_Wq, L0_xattn_bq, L0_xattn_Wk, L0_xattn_bk, L0_xattn_Wv, L0_xattn_bv, L0_xattn_Wo, L0_xattn_bo, L0_xattn_gamma, L0_xattn_beta, L1_xattn_Wq, L1_xattn_Wk, L1_xattn_Wv, L1_xattn_Wo, L1_xattn_ln_gamma, L1_xattn_ln_beta, L1_xattn_gate):
    import jax
    import jax.numpy as jnp

    def _L0_xattn_ref(hidden_state, encoder_hidden_state, encoder_attention_mask, Wq, bq, Wk, bk, Wv, bv, Wo, bo, gamma, beta):
        import jax, jax.numpy as jnp
        import numpy as np
        H = 512
        NH = 32
        KVH = 8
        HD = H // NH
        GROUPS = NH // KVH
        EPS = 1e-06
        B, L, S = (4, 256, 256)

        def _gqa_forward(hidden_state, encoder_hidden_state, encoder_attention_mask, Wq, bq, Wk, bk, Wv, bv, Wo, bo, gamma, beta):
            b, l, _ = hidden_state.shape
            s = encoder_hidden_state.shape[1]
            q = hidden_state @ Wq + bq
            k = encoder_hidden_state @ Wk + bk
            v = encoder_hidden_state @ Wv + bv
            q = q.reshape(b, l, KVH, GROUPS, HD).transpose(0, 2, 3, 1, 4)
            k = k.reshape(b, s, KVH, HD).transpose(0, 2, 1, 3)
            v = v.reshape(b, s, KVH, HD).transpose(0, 2, 1, 3)
            scale = 1.0 / jnp.sqrt(jnp.asarray(HD, q.dtype))
            scores = jnp.einsum('bkgld,bksd->bkgls', q, k) * scale
            scores = scores + encoder_attention_mask[:, :, None, :, :]
            attn = jax.nn.softmax(scores, axis=-1)
            out = jnp.einsum('bkgls,bksd->bkgld', attn, v)
            out = out.transpose(0, 3, 1, 2, 4).reshape(b, l, H)
            out = out @ Wo + bo
            x = out + hidden_state
            mu = jnp.mean(x, axis=-1, keepdims=True)
            var = jnp.var(x, axis=-1, keepdims=True)
            return (x - mu) * jax.lax.rsqrt(var + EPS) * gamma + beta
        return _gqa_forward(hidden_state, encoder_hidden_state, encoder_attention_mask, Wq, bq, Wk, bk, Wv, bv, Wo, bo, gamma, beta)

    def _L1_xattn_ref(hidden_states, audio_kv, audio_attention_mask, Wq, Wk, Wv, Wo, ln_gamma, ln_beta, gate):
        import jax, jax.numpy as jnp
        import numpy as np
        HIDDEN = 512
        HEADS = 16
        HEAD_DIM = HIDDEN // HEADS
        LN_EPS = 1e-05
        GATE_INIT = 0.5

        def _layer_norm(x, gamma, beta):
            mu = jnp.mean(x, axis=-1, keepdims=True)
            var = jnp.mean(jnp.square(x - mu), axis=-1, keepdims=True)
            return (x - mu) * jax.lax.rsqrt(var + LN_EPS) * gamma + beta
        B, Tt, D = hidden_states.shape
        Ta = audio_kv.shape[1]
        scale = HEAD_DIM ** (-0.5)
        a = _layer_norm(audio_kv, ln_gamma, ln_beta)
        Q = (hidden_states @ Wq.T).reshape(B, Tt, HEADS, HEAD_DIM).transpose(0, 2, 1, 3)
        K = (a @ Wk.T).reshape(B, Ta, HEADS, HEAD_DIM).transpose(0, 2, 1, 3)
        V = (a @ Wv.T).reshape(B, Ta, HEADS, HEAD_DIM).transpose(0, 2, 1, 3)
        scores = jnp.einsum('bhtd,bhsd->bhts', Q, K) * scale
        mask = audio_attention_mask[:, None, None, :]
        scores = jnp.where(mask, scores, jnp.float32(-jnp.inf))
        attn = jax.nn.softmax(scores, axis=-1)
        out = jnp.einsum('bhts,bhsd->bhtd', attn, V)
        out = out.transpose(0, 2, 1, 3).reshape(B, Tt, D)
        out = out @ Wo.T
        return hidden_states + jnp.tanh(gate) * out
    x = _L0_xattn_ref(x, ctx_2048, mask_Bx1xSxS2_ff0, L0_xattn_Wq, L0_xattn_bq, L0_xattn_Wk, L0_xattn_bk, L0_xattn_Wv, L0_xattn_bv, L0_xattn_Wo, L0_xattn_bo, L0_xattn_gamma, L0_xattn_beta)
    x = _L1_xattn_ref(x, ctx_2048, mask_BxS2_bf1, L1_xattn_Wq, L1_xattn_Wk, L1_xattn_Wv, L1_xattn_Wo, L1_xattn_ln_gamma, L1_xattn_ln_beta, L1_xattn_gate)
    return x

_drawn_inputs = setup_inputs


def setup_inputs(seed=0):
    import zlib

    import numpy as np

    out = dict(_drawn_inputs(seed))
    spreads = {'L0_xattn_bq': (0.0, 0.8),
     'L0_xattn_bk': (0.0, 0.8),
     'L0_xattn_bv': (0.0, 0.1),
     'L0_xattn_bo': (0.0, 0.1),
     'L0_xattn_gamma': (1.0, 0.2),
     'L0_xattn_beta': (0.0, 0.1),
     'L1_xattn_ln_gamma': (1.0, 0.6),
     'L1_xattn_ln_beta': (0.0, 0.8)}
    factors = {'L0_xattn_Wq': 7.631, 'L0_xattn_Wk': 7.468, 'L1_xattn_Wq': 8.0, 'L1_xattn_Wk': 8.0}
    for name, (base, spread) in spreads.items():
        noise = np.random.default_rng([zlib.crc32(name.encode()), seed]).standard_normal(out[name].shape)
        drawn = base * np.exp(spread * noise) if base else spread * noise
        out[name] = jnp.asarray(drawn.astype(out[name].dtype))
    for name, factor in factors.items():
        out[name] = (out[name] * factor).astype(out[name].dtype)
    return out
```

```python
from contextlib import ExitStack

import concourse.bass as bass
from concourse import mybir

F32 = mybir.dt.float32
F32R = mybir.dt.float32r
U8 = mybir.dt.uint8
ALU = mybir.AluOpType
ACT = mybir.ActivationFunctionType

P = 128
BIG = 3.0e38


def wait_from(engine, semaphore, count):
    if not isinstance(count, int) or count > 0:
        engine.wait_ge(semaphore, count)


def two_layer_cross_attention(nc, x_rows, x_cols, ctx_rows, ctx_cols, mask0, mask1,
                              wq0, wk0, wv0, wo0, bq0, bk0, bv0, bo0, gamma0, beta0,
                              wq1, wk1, wv1, wo1, gamma1, beta1, gate, out):
    NB, T, D = x_rows.shape
    S = ctx_rows.shape[1]
    C = D // P
    KVH, HD0 = 8, 16
    GR = D // (KVH * HD0)
    HD1 = 32
    SC = 3
    SP = -(-S // SC)
    SE = S + (S & 1)
    SW = 364
    NH = 48
    HALF = 8
    NHALF = NH // HALF
    NJ = 4
    EPS0, EPS1 = 1e-6, 1e-5
    SCALE0, SCALE1 = HD0 ** -0.5, HD1 ** -0.5
    assert SC * SP <= SW and D == C * P and KVH * HD0 == P and SE <= 512

    with ExitStack() as ctx:
        def sb(name, shape, dt=F32):
            return ctx.enter_context(nc.sbuf_tensor(name, shape, dt))

        def sem(name):
            return ctx.enter_context(nc.semaphore(name))

        WQ0 = sb("WQ0", [P, C, D])
        WO0 = sb("WO0", [P, C, D])
        WQ1 = sb("WQ1", [P, C, D])
        WO1 = sb("WO1", [P, C, D])
        WK0h, WK0l = sb("WK0h", [P, C, P], F32R), sb("WK0l", [P, C, P], F32R)
        WV0h, WV0l = sb("WV0h", [P, C, P], F32R), sb("WV0l", [P, C, P], F32R)
        WK1h, WK1l = sb("WK1h", [P, C, D], F32R), sb("WK1l", [P, C, D], F32R)
        WV1h, WV1l = sb("WV1h", [P, C, D], F32R), sb("WV1l", [P, C, D], F32R)
        BQ0, BK0 = sb("BQ0", [P, GR]), sb("BK0", [P, 1])
        BV0 = sb("BV0", [P, SC, P])
        BO0, G0, B0 = sb("BO0", [P, D]), sb("G0", [P, D]), sb("B0", [P, D])
        G1, B1 = sb("G1", [P, C]), sb("B1", [P, C])
        GT = sb("GT", [P, 2])
        ident = sb("ident", [P, P])
        mhalf = sb("mhalf", [P, SC])

        CT = sb("CT", [P, C, SW])
        TH, TL = sb("TH", [P, C, SW], F32R), sb("TL", [P, C, SW], F32R)
        NAT = sb("NAT", [P, SC, D])
        AT = sb("AT", [P, C, SW])
        CST, CMV, CVE, CRS = sb("CST", [P, SC, 6]), sb("CMV", [P, SC, 2]), sb("CVE", [P, SC]), sb("CRS", [P, SC])
        K1h, K1l = sb("K1h", [P, C, SW], F32R), sb("K1l", [P, C, SW], F32R)
        V1 = sb("V1", [P, SC, D])
        KHL = sb("KHL", [P, 2, SW], F32R)
        K0S = sb("K0S", [P, 4, SW], F32R)
        V0P = sb("V0P", [P, SC, KVH, 3 * HD0])
        XT = sb("XT", [P, C, T])
        XN = sb("XN", [P, D])
        QHL = sb("QHL", [P, 2, GR, T], F32R)
        Q0S = sb("Q0S", [P, 4, GR, T], F32R)
        MK0, MU, MK1 = sb("MK0", [P, S]), sb("MU", [P, S], U8), sb("MK1", [P, S])
        PR = sb("PR", [P, 3, SW])
        MN, SM = sb("MN", [P, NH]), sb("SM", [P, NH])
        PT = sb("PT", [P, 2, HALF, SC * T])
        AT_flat = AT[:, :, :].rearrange("p a b -> p (a b)")
        PT_flat = PT[:, :, :, :].rearrange("p a b c -> p (a b c)")
        SX = sb("SX", [P, C, P])
        RI = sb("RI", [P, C * T])
        OT0, OT1 = sb("OT0", [P, C, T]), sb("OT1", [P, C, T])
        R0, Y = sb("R0", [P, D]), sb("Y", [P, D])
        YST, YMV, YVE, YRS = sb("YST", [P, 6]), sb("YMV", [P, 2]), sb("YVE", [P, 1]), sb("YRS", [P, 1])
        YT = sb("YT", [P, C, T])
        Q1h, Q1l = sb("Q1h", [P, C, T], F32R), sb("Q1l", [P, C, T], F32R)
        OUT = sb("OUT", [P, D])

        k_scr = nc.dram_tensor("k_scr", (2, P, SW), F32, kind="Internal").ap()
        q_scr = nc.dram_tensor("q_scr", (2, P, GR * T), F32, kind="Internal").ap()

        SCO = ctx.enter_context(nc.psum_tensor("SCO", [P, 3, 512], F32))
        TP = ctx.enter_context(nc.psum_tensor("TP", [P, 2, 512], F32))
        OA = ctx.enter_context(nc.psum_tensor("OA", [P, 512], F32))
        PJ = ctx.enter_context(nc.psum_tensor("PJ", [P, 2, 512], F32))

        l_w0, l_w1, l_q1, l_o, l_sm = sem("l_w0"), sem("l_w1"), sem("l_q1"), sem("l_o"), sem("l_sm")
        l_ct, l_nat, l_xt, l_xn = sem("l_ct"), sem("l_nat"), sem("l_xt"), sem("l_xn")
        l_mk0, l_mk1 = sem("l_mk0"), sem("l_mk1")
        kst, kld, qst, qld, ost = sem("kst"), sem("kld"), sem("qst"), sem("qld"), sem("ost")
        w_h, w_split, w_q0, ready = sem("w_h"), sem("w_split"), sem("w_q0"), sem("ready")
        gate_t, w_q0b, ready_parts, nat_zero = sem("gate_t"), sem("w_q0b"), sem("ready_parts"), sem("nat_zero")
        ident0 = sem("ident0")
        ct_h, ct_l = sem("ct_h"), sem("ct_l")
        k0_mm, k0_h, k0_l = sem("k0_mm"), sem("k0_h"), sem("k0_l")
        q0_mm, q0_h, q0_l = sem("q0_mm"), sem("q0_h"), sem("q0_l")
        v0_mm, v0_ev = sem("v0_mm"), sem("v0_ev")
        c_st, c_mv, c_ve, c_rs, c_nrm = sem("c_st"), sem("c_mv"), sem("c_ve"), sem("c_rs"), sem("c_nrm")
        at_mm, at_ev, at_h, at_l = sem("at_mm"), sem("at_ev"), sem("at_h"), sem("at_l")
        k1_mm, k1_h, k1_l = sem("k1_mm"), sem("k1_h"), sem("k1_l")
        v1_mm, v1_ev = sem("v1_mm"), sem("v1_ev")
        mk1_a, mk1_b = sem("mk1_a"), sem("mk1_b")
        scored, shifted, prob = sem("scored"), sem("shifted"), sem("prob")
        pt_mm, pt_even, pt_odd = sem("pt_mm"), sem("pt_even"), sem("pt_odd")
        sums_x = sem("sums_x")
        pv, sums_t, inv, attn = sem("pv"), sem("sums_t"), sem("inv"), sem("attn")
        xb, out0_mm, res, y_st, y_mv, y_ve, y_rs = (sem("xb"), sem("out0_mm"), sem("res"), sem("y_st"),
                                                    sem("y_mv"), sem("y_ve"), sem("y_rs"))
        y_n, y_g, y_ok, yt_mm, yt_ev = sem("y_n"), sem("y_g"), sem("y_ok"), sem("yt_mm"), sem("yt_ev")
        q1_mm, q1_h, q1_l, out1_mm, fin = sem("q1_mm"), sem("q1_h"), sem("q1_l"), sem("out1_mm"), sem("fin")

        met_dve, met_pool, met_sp = sem("met_dve"), sem("met_pool"), sem("met_sp")
        NLOAD_K = 8

        block = ctx.enter_context(nc.Block())

        @block.sync
        def _(sp):
            def load_ctx_cols(q):
                sp.dma_start(CT[:, :, 0:S], ctx_cols[q]).then_inc(l_ct, 16)

            def load_ctx_rows(q):
                full = (SC - 1) * SP
                sp.dma_start(NAT[0:SP, 0:SC - 1, :],
                             ctx_rows[q, 0:full, :].rearrange("(c p) d -> p c d", p=SP)).then_inc(l_nat, 16)
                sp.dma_start(NAT[0:S - full, SC - 1, :], ctx_rows[q, full:S, :]).then_inc(l_nat, 16)

            def shuffle_keys(q):
                sp.wait_ge(k0_h, q + 1)
                sp.wait_ge(k0_l, q + 1)
                for hl in range(2):
                    sp.dma_start(k_scr[hl], KHL[:, hl, :].bitcast(F32)).then_inc(kst, 16)
                sp.wait_ge(kst, 32 * q + 32)
                wait_from(sp, scored, NH * q - 16)
                for par in range(2):
                    for e in range(2):
                        for hl in range(2):
                            at = 64 * par + 32 * e + 16 * hl
                            src = k_scr[hl, 64 * par:64 * par + 64, :].rearrange("(d i) s -> d i s", i=4)
                            sp.dma_start(K0S[at:at + 16, :, :].bitcast(F32), src).then_inc(kld, 16)

            def shuffle_queries(q):
                sp.wait_ge(q0_h, 4 * q + 4)
                sp.wait_ge(q0_l, 4 * q + 4)
                for hl in range(2):
                    sp.dma_start(q_scr[hl], QHL[:, hl, :, :].bitcast(F32)).then_inc(qst, 16)
                sp.wait_ge(qst, 32 * q + 32)
                for par in range(2):
                    for e in range(2):
                        for hl in range(2):
                            at = 64 * par + 32 * hl + 16 * e
                            src = q_scr[hl, 64 * par:64 * par + 64, :].rearrange("(d i) s -> d i s", i=4)
                            dst = Q0S[at:at + 16, :, :, :].bitcast(F32).rearrange("d i g t -> d i (g t)")
                            sp.dma_start(dst, src).then_inc(qld, 16)

            sp.dma_start(CT[:, :, 0:S], ctx_cols[0]).then_inc(l_ct, 16)
            for n, w in enumerate((wk0, wv0)):
                sp.dma_start(AT_flat[:, n * C * P:(n + 1) * C * P], w.rearrange("p c n -> p (c n)")).then_inc(l_w0, 16)
            sp.dma_start(XT[:, :, :], x_cols[0]).then_inc(l_xt, 16)
            sp.dma_start(WQ0[:, :, :], wq0).then_inc(l_q1, 16)
            for dst, src in ((BQ0, bq0), (BK0, bk0), (G1, gamma1), (B1, beta1)):
                sp.dma_start(dst[:, :], src).then_inc(l_sm, 16)
            for c in range(SC):
                sp.dma_start(BV0[:, c, :], bv0.partition_broadcast(P)).then_inc(l_sm, 16)
            for dst, src in ((BO0, bo0), (G0, gamma0), (B0, beta0)):
                sp.dma_start(dst[:, :], src.partition_broadcast(P)).then_inc(l_sm, 16)
            sp.dma_start(GT[:, 0:1], gate.partition_broadcast(P)).then_inc(l_sm, 16)
            sp.wait_ge(nat_zero, 1)
            load_ctx_rows(0)
            for n, w in enumerate((wk1, wv1)):
                sp.dma_start(PT_flat[:, n * C * D:(n + 1) * C * D], w.rearrange("p c n -> p (c n)")).then_inc(l_w1, 16)
            sp.dma_start(MK0[0:T, :], mask0[0]).then_inc(l_mk0, 16)
            sp.dma_start(MU[0:T, :], mask1[0].partition_broadcast(T)).then_inc(l_mk1, 16)
            sp.dma_start(XN[0:T, :], x_rows[0]).then_inc(l_xn, 16)
            sp.dma_start(WO0[:, :, :], wo0).then_inc(l_o, 16)
            sp.dma_start(WQ1[:, :, :], wq1).then_inc(l_o, 16)
            sp.dma_start(WO1[:, :, :], wo1).then_inc(l_o, 16)
            shuffle_keys(0)
            shuffle_queries(0)

            def batch(b, more):
                if more:
                    sp.wait_ge(ct_h, b + 1)
                    sp.wait_ge(ct_l, b + 1)
                    load_ctx_cols(b + 1)
                    sp.wait_ge(q0_mm, b + 1)
                    sp.dma_start(XT[:, :, :], x_cols[b + 1]).then_inc(l_xt, 16)
                    sp.wait_ge(at_mm, 4 * b + 4)
                    load_ctx_rows(b + 1)
                    sp.wait_ge(mk1_a, b + 1)
                    sp.sem_inc(met_sp, 1)
                    sp.dma_start(MU[0:T, :], mask1[b + 1].partition_broadcast(T)).then_inc(l_mk1, 16)
                    sp.wait_ge(shifted, NH * b + 32)
                    sp.dma_start(MK0[0:T, :], mask0[b + 1]).then_inc(l_mk0, 16)
                    shuffle_keys(b + 1)
                    sp.wait_ge(res, b + 1)
                    sp.dma_start(XN[0:T, :], x_rows[b + 1]).then_inc(l_xn, 16)
                    shuffle_queries(b + 1)
                sp.wait_ge(fin, b + 1)
                sp.dma_start(out[b], OUT[0:T, :]).then_inc(ost, 16)

            batch(0, True)
            with sp.Fori(1, NB - 1) as b:
                batch(b, True)
            batch(NB - 1, False)
            sp.wait_ge(ost, 16 * NB)

        @block.tensor
        def _(pe):
            def mm3(dst, wh, wl, xh, xl, start, stop):
                pe.matmul(dst, wh, xh, start=start, stop=False)
                pe.matmul(dst, wl, xh, start=False, stop=False)
                return pe.matmul(dst, wh, xl, start=False, stop=stop)

            def keys0():
                for c in range(C):
                    last = mm3(PJ[:, 1, 0:SW], WK0h[:, c, :], WK0l[:, c, :], TH[:, c, :], TL[:, c, :],
                               c == 0, c == C - 1)
                last.then_inc(k0_mm, 1)

            def queries0():
                for g in range(GR):
                    for c in range(C):
                        last = pe.matmul(PJ[:, 1, g * T:(g + 1) * T], WQ0[:, c, g * P:(g + 1) * P],
                                         XT[:, c, :], start=c == 0, stop=c == C - 1)
                last.then_inc(q0_mm, 1)

            def values0():
                for s in range(SC):
                    rows = slice(s * SP, (s + 1) * SP)
                    for c in range(C):
                        last = mm3(PJ[0:SP, 0, s * P:(s + 1) * P], TH[:, c, rows], TL[:, c, rows],
                                   WV0h[:, c, :], WV0l[:, c, :], c == 0, c == C - 1)
                last.then_inc(v0_mm, 1)

            def score(b, k):
                dst = SCO[0:T, k % 3, 0:SE]
                if k < 32:
                    G, gh, gl, j = k // 16, k // 8 % 2, k // 4 % 2, k % 4
                    pe.matmul(dst, Q0S[64 * G:64 * G + 64, j, 2 * gh + gl, :], K0S[64 * G:64 * G + 64, j, 0:SE],
                              start=True, stop=True).then_inc(scored, 1)
                else:
                    m, j = (k - 32) // 4, k % 4
                    r = slice(32 * j, 32 * j + 32)
                    mm3(dst, Q1h[r, m, :], Q1l[r, m, :], K1h[r, m, 0:SE], K1l[r, m, 0:SE], True, True)\
                        .then_inc(scored, 1)

            def transpose_probs(b, k):
                pe.wait_ge(prob, NH * b + k + 1)
                for c in range(SC):
                    last = pe.transpose(TP[0:SP, k % 2, c * T:(c + 1) * T], PR[0:T, k % 3, c * SP:(c + 1) * SP],
                                        ident[0:T, 0:T])
                last.then_inc(pt_mm, 1)

            def free_tp(b, k):
                if k >= 2:
                    pe.wait_ge(pt_even if k % 2 == 0 else pt_odd, 24 * b + k // 2)
                else:
                    wait_from(pe, pt_even if k % 2 == 0 else pt_odd, 24 * b)

            def out_half(b, h):
                pe.wait_ge(pt_even, 24 * b + 4 * h + 4)
                pe.wait_ge(pt_odd, 24 * b + 4 * h + 4)
                if h % 2 == 0:
                    wait_from(pe, attn, 3 * b + h // 2)
                if h < 4:
                    G, gh = h // 2, h % 2
                    for c in range(SC):
                        for j in range(NJ):
                            lhs = V0P[0:SP, c, 4 * G + j, (HD0, 0)[gh]:(HD0, 0)[gh] + 32]
                            rhs = PT[0:SP, h % 2, :, c * T:(c + 1) * T].rearrange("p (a j) t -> p a j t", j=NJ)[:, :, j, :]
                            last = pe.matmul(OA[32 * j:32 * j + 32, 0:2 * T], lhs, rhs,
                                             start=gh == 0 and c == 0, stop=gh == 1 and c == SC - 1)
                else:
                    for ml in range(2):
                        m = 2 * (h - 4) + ml
                        for c in range(SC):
                            for j in range(NJ):
                                head = 4 * m + j
                                last = pe.matmul(OA[32 * j:32 * j + 32, m * T:(m + 1) * T],
                                                 V1[0:SP, c, head * HD1:(head + 1) * HD1],
                                                 PT[0:SP, h % 2, 4 * ml + j, c * T:(c + 1) * T],
                                                 start=c == 0, stop=c == SC - 1)
                last.then_inc(pv, 1)

            def sums_transposed(b, u):
                dst = OA[:, 2 * T:4 * T] if u < 2 else PJ[:, 0, :]
                pe.wait_ge(sums_x, 3 * b + u + 1)
                for m in range(2 if u < 2 else C):
                    last = pe.transpose(dst[:, m * T:(m + 1) * T], SX[0:T, m, :], ident[0:T, 0:T])
                last.then_inc(sums_t, 1)

            def dense(dst, src, W, signal):
                for c in range(C):
                    last = pe.matmul(dst, src[:, c, :], W[:, c, :], start=c == 0, stop=c == C - 1)
                last.then_inc(signal, 1)

            def piece(b, k):
                if k < 4:
                    if k == 0:
                        pe.wait_ge(c_nrm, 3 * b + 3)
                        pe.wait_ge(v0_ev, b + 1)
                        wait_from(pe, inv, 3 * b)
                    elif k == 1:
                        pe.wait_ge(q0_l, 4 * b + 4)
                        wait_from(pe, fin, b)
                    else:
                        pe.wait_ge(at_ev, 4 * b + k - 1)
                    for s in range(SC):
                        last = pe.transpose(PJ[:, k % 2, s * SP:(s + 1) * SP], NAT[0:SP, s, k * P:(k + 1) * P],
                                            ident[0:SP, 0:SP])
                    last.then_inc(at_mm, 1)
                elif k < 20:
                    m, c = (k - 4) // 4, k % 4
                    if c == 0:
                        if m < 2:
                            pe.wait_ge(at_ev, 4 * b + m + 3)
                        else:
                            pe.wait_ge(k1_l, 4 * b + m - 1)
                    if m == 0:
                        pe.wait_ge(at_h, 4 * b + c + 1)
                        pe.wait_ge(at_l, 4 * b + c + 1)
                    cols = slice(m * P, (m + 1) * P)
                    last = mm3(PJ[:, m % 2, 0:SW], WK1h[:, c, cols], WK1l[:, c, cols], TH[:, c, :], TL[:, c, :],
                               c == 0, c == C - 1)
                    if c == C - 1:
                        last.then_inc(k1_mm, 1)
                else:
                    s, c = (k - 20) // 4, k % 4
                    if c == 0:
                        if s < 2:
                            pe.wait_ge(k1_l, 4 * b + s + 3)
                        else:
                            pe.wait_ge(v1_ev, 3 * b + 1)
                    rows = slice(s * SP, (s + 1) * SP)
                    last = mm3(PJ[0:SP, s % 2, :], TH[:, c, rows], TL[:, c, rows], WV1h[:, c, :], WV1l[:, c, :],
                               c == 0, c == C - 1)
                    if c == C - 1:
                        last.then_inc(v1_mm, 1)

            pe.wait_ge(ready, 1)
            pe.wait_ge(w_split, 2)
            pe.wait_ge(ct_h, 1)
            pe.wait_ge(ct_l, 1)
            keys0()
            pe.wait_ge(w_q0, 1)
            pe.wait_ge(l_xt, 16)
            pe.wait_ge(k0_l, 1)
            queries0()
            values0()
            pe.wait_ge(w_split, 4)
            pe.wait_ge(l_o, 48)

            def batch(b, more):
                pe.wait_ge(kld, 16 * NLOAD_K * b + 16 * NLOAD_K)
                pe.wait_ge(qld, 16 * NLOAD_K * b + 16 * NLOAD_K)
                for k in range(34):
                    if k < 32:
                        if k < 3:
                            wait_from(pe, prob, NH * b)
                        else:
                            pe.wait_ge(prob, NH * b + k - 2)
                        score(b, k)
                        piece(b, k)
                    if k >= 2:
                        free_tp(b, k - 2)
                        transpose_probs(b, k - 2)
                    if k in (11, 19, 27):
                        out_half(b, (k - 11) // 8)
                    if k == 19:
                        sums_transposed(b, 0)
                out_half(b, 3)
                sums_transposed(b, 1)
                if more:
                    pe.wait_ge(ct_h, b + 2)
                    pe.wait_ge(ct_l, b + 2)
                    pe.wait_ge(v1_ev, 3 * b + 2)
                    keys0()
                pe.wait_ge(v1_ev, 3 * b + 3)
                pe.wait_ge(attn, 3 * b + 2)
                dense(PJ[0:T, 0, :], OT0, WO0, out0_mm)
                if more:
                    pe.wait_ge(k0_l, b + 2)
                    pe.wait_ge(l_xt, 16 * b + 32)
                    queries0()
                    pe.wait_ge(res, b + 1)
                    values0()
                    pe.wait_ge(q0_l, 4 * b + 8)
                else:
                    pe.wait_ge(v1_ev, 3 * b + 2)
                pe.wait_ge(y_ok, b + 1)
                for c in range(C):
                    last = pe.transpose(PJ[:, 1, c * T:(c + 1) * T], Y[0:T, c * P:(c + 1) * P], ident[0:T, 0:T])
                last.then_inc(yt_mm, 1)
                if more:
                    pe.wait_ge(v0_ev, b + 2)
                pe.wait_ge(res, b + 1)
                pe.wait_ge(yt_ev, b + 1)
                for m in range(C):
                    for c in range(C):
                        last = pe.matmul(PJ[:, 0, m * T:(m + 1) * T], WQ1[:, c, m * P:(m + 1) * P], YT[:, c, :],
                                         start=c == 0, stop=c == C - 1)
                last.then_inc(q1_mm, 1)
                pe.wait_ge(q1_h, b + 1)
                pe.wait_ge(q1_l, b + 1)
                for k in range(32, NH + 2):
                    if k < NH:
                        pe.wait_ge(prob, NH * b + k - 2)
                        score(b, k)
                    if k >= 34:
                        free_tp(b, k - 2)
                        transpose_probs(b, k - 2)
                    if k == 43:
                        out_half(b, 4)
                sums_transposed(b, 2)
                out_half(b, 5)
                pe.wait_ge(attn, 3 * b + 3)
                dense(PJ[0:T, 1, :], OT1, WO1, out1_mm)

            batch(0, True)
            with pe.Fori(1, NB - 1) as b:
                batch(b, True)
            batch(NB - 1, False)

        @block.vector
        def _(dve):
            def split_ctx(q):
                dve.wait_ge(l_ct, 16 * q + 16)
                dve.tensor_copy(TH[:, :, :], CT[:, :, :]).then_inc(ct_h, 1)

            def keys0_low(q):
                dve.wait_ge(k0_h, q + 1)
                dve.scalar_tensor_tensor(out=KHL[:, 1, :], in0=PJ[:, 1, 0:SW], scalar=BK0[:, 0:1],
                                         in1=KHL[:, 0, :].bitcast(F32), op0=ALU.add, op1=ALU.subtract)\
                    .then_inc(k0_l, 1)

            def queries0_low(q):
                for g in range(GR):
                    dve.wait_ge(q0_h, 4 * q + 4)
                    dve.scalar_tensor_tensor(out=QHL[:, 1, g, :], in0=PJ[:, 1, g * T:(g + 1) * T],
                                             scalar=BQ0[:, g:g + 1], in1=QHL[:, 0, g, :].bitcast(F32),
                                             op0=ALU.add, op1=ALU.subtract).then_inc(q0_l, 1)

            def values0(q):
                dve.wait_ge(v0_mm, q + 1)
                dve.tensor_tensor(V0P[0:SP, :, :, HD0:2 * HD0],
                                  PJ[0:SP, 0, 0:SC * P].rearrange("p (s h d) -> p s h d", s=SC, h=KVH),
                                  BV0[0:SP, :, :].rearrange("p s (h d) -> p s h d", h=KVH), ALU.add)\
                    .then_inc(v0_ev, 1)

            def ctx_stats(q, s):
                if s == 0:
                    dve.wait_ge(l_nat, 32 * q + 32)
                dve.bn_stats(CST[0:SP, s, :], NAT[0:SP, s, :]).then_inc(c_st, 1)

            def ctx_mean(q):
                dve.wait_ge(c_st, 3 * q + 3)
                dve.sem_inc(met_dve, 1)
                for s in range(SC):
                    dve.bn_aggr(CMV[0:SP, s, :], CST[0:SP, s, :]).then_inc(c_mv, 1)

            def ctx_normalise(q, s):
                dve.wait_ge(c_rs, q + 1)
                dve.tensor_scalar(NAT[0:SP, s, :], NAT[0:SP, s, :], CMV[0:SP, s, 0:1], CRS[0:SP, s:s + 1],
                                  ALU.subtract, ALU.mult).then_inc(c_nrm, 1)

            def shift(b, k):
                dve.wait_ge(scored, NH * b + k + 1)
                dve.sem_inc(met_dve, 1)
                bank = SCO[0:T, k % 3, 0:S]
                mask, scale = (MK0, -1.0) if k < 32 else (MK1, -SCALE1)
                dve.tensor_tensor_reduce(out=bank, in0=bank, in1=mask[0:T, :], scale=scale, scalar=3.4e38,
                                         op0=ALU.add, op1=ALU.min, accum_out=MN[0:T, k:k + 1]).then_inc(shifted, 1)

            def probs_out(b, k):
                dve.wait_ge(pt_mm, NH * b + k + 1)
                h = k // HALF
                if k % HALF == 1:
                    wait_from(dve, pv, NHALF * b + h - 1)
                dve.tensor_copy(PT[0:SP, h % 2, k % HALF, :], TP[0:SP, k % 2, 0:SC * T]).then_inc(pt_odd, 1)

            def repeat_sums(b, u):
                dve.wait_ge(prob, NH * b + 16 * u + 16)
                wait_from(dve, sums_t, 3 * b + u)
                sums = SM[0:T, 16 * u:16 * u + 16]
                if u < 2:
                    src = sums.rearrange("p (a g j) -> p g j a", a=2, g=2).unsqueeze(4).to_broadcast([T, 2, NJ, 2, HD0])
                    dve.tensor_copy(SX[0:T, 0:2, :].rearrange("p g (j a d) -> p g j a d", j=NJ, a=2), src)\
                        .then_inc(sums_x, 1)
                else:
                    src = sums.unsqueeze(2).to_broadcast([T, 16, HD1])
                    dve.tensor_copy(SX[0:T, :, :].rearrange("p m (j d) -> p (m j) d", j=NJ), src).then_inc(sums_x, 1)

            def unit_sums(b, u, width):
                dve.wait_ge(sums_t, 3 * b + u + 1)
                src = OA[:, 2 * T:4 * T] if u < 2 else PJ[:, 0, 0:C * T]
                dve.reciprocal(RI[:, 0:width], src).then_inc(inv, 1)

            def unit_outputs(b, u):
                dve.wait_ge(pv, NHALF * b + 2 * u + 2)
                dve.wait_ge(inv, 3 * b + u + 1)
                if u < 2:
                    cols = slice(0, 2 * T)
                    dst, n = OT0[:, 2 * u:2 * u + 2, :].rearrange("p c t -> p (c t)"), 2 * T
                else:
                    cols = slice(0, C * T)
                    dst, n = OT1[:, :, :].rearrange("p c t -> p (c t)"), C * T
                dve.tensor_tensor(dst, OA[:, cols], RI[:, 0:n], ALU.mult).then_inc(attn, 1)

            dve.memset(CT[:, :, S:SW], 0.0).then_inc(ready_parts, 1)
            dve.memset(NAT[:, :, :], 0.0).then_inc(nat_zero, 1)
            dve.memset(V0P[:, :, :, :], 0.0).then_inc(ready_parts, 1)
            dve.memset(PR[:, :, :], 0.0).then_inc(ready_parts, 1)
            dve.memset(mhalf[:, :], -0.5).then_inc(ready_parts, 1)
            dve.memset(ident[:, :], 1.0).then_inc(ident0, 1)
            dve.wait_ge(ready_parts, 4)
            dve.wait_ge(l_w0, 32)
            first = ((WK0h, WK0l), (WV0h, WV0l))
            for n, (wh, _) in enumerate(first):
                dve.tensor_copy(wh[:, :, :].rearrange("p c n -> p (c n)"), AT_flat[:, n * C * P:(n + 1) * C * P])\
                    .then_inc(w_h, 1)
            split_ctx(0)
            dve.wait_ge(w_h, 2)
            for n, (wh, wl) in enumerate(first):
                dve.tensor_tensor(wl[:, :, :].rearrange("p c n -> p (c n)"), AT_flat[:, n * C * P:(n + 1) * C * P],
                                  wh[:, :, :].bitcast(F32).rearrange("p c n -> p (c n)"), ALU.subtract)\
                    .then_inc(w_split, 1)
            dve.wait_ge(l_sm, 16 * 11)
            dve.wait_ge(k0_mm, 1)
            keys0_low(0)
            queries0_low(0)
            values0(0)
            for s in range(SC):
                ctx_stats(0, s)
            ctx_mean(0)
            dve.wait_ge(l_w1, 32)
            for n, (wh, wl) in enumerate(((WK1h, WK1l), (WV1h, WV1l))):
                part = PT_flat[:, n * C * D:(n + 1) * C * D]
                dve.tensor_copy(wh[:, :, :].rearrange("p c n -> p (c n)"), part).then_inc(w_h, 1)
                dve.wait_ge(w_h, 3 + n)
                dve.tensor_tensor(wl[:, :, :].rearrange("p c n -> p (c n)"), part,
                                  wh[:, :, :].bitcast(F32).rearrange("p c n -> p (c n)"), ALU.subtract)\
                    .then_inc(w_split, 1)
            for s in range(SC):
                ctx_normalise(0, s)
            dve.wait_ge(w_split, 4)

            def batch(b, more):
                dve.wait_ge(l_mk0, 16 * b + 16)
                for k in range(35):
                    if k < 32:
                        shift(b, k)
                    if k >= 3 and (k - 3) % 2 == 1:
                        probs_out(b, k - 3)
                    if k < 4:
                        dve.wait_ge(at_mm, 4 * b + k + 1)
                        wait_from(dve, at_l, 4 * b)
                        wait_from(dve, at_h, 4 * b)
                        dve.tensor_scalar(AT[:, k, 0:SC * SP], PJ[:, k % 2, 0:SC * SP], G1[:, k:k + 1], B1[:, k:k + 1],
                                          ALU.mult, ALU.add).then_inc(at_ev, 1)
                    if k in (9, 13, 17, 21):
                        m = (k - 9) // 4
                        dve.wait_ge(k1_h, 4 * b + m + 1)
                        dve.tensor_tensor(K1l[:, m, :], PJ[:, m % 2, 0:SW], K1h[:, m, :].bitcast(F32),
                                          ALU.subtract).then_inc(k1_l, 1)
                    if k == 18:
                        repeat_sums(b, 0)
                    if k == 21:
                        unit_sums(b, 0, 2 * T)
                    if k == 22:
                        unit_outputs(b, 0)
                    if more and k in (12, 14, 16):
                        ctx_stats(b + 1, (k - 12) // 2)
                    if more and k == 18:
                        ctx_mean(b + 1)
                    if more and k in (24, 25, 26):
                        ctx_normalise(b + 1, k - 24)
                    if more and k == 33:
                        dve.wait_ge(v1_mm, 3 * b + 3)
                        split_ctx(b + 1)
                    if k == 33:
                        repeat_sums(b, 1)
                unit_sums(b, 1, 2 * T)
                unit_outputs(b, 1)
                if more:
                    keys0_low(b + 1)
                dve.wait_ge(out0_mm, b + 1)
                dve.wait_ge(xb, b + 1)
                dve.tensor_tensor(R0[0:T, :], PJ[0:T, 0, :], XN[0:T, :], ALU.add).then_inc(res, 1)
                dve.wait_ge(res, b + 1)
                dve.bn_stats(YST[0:T, :], R0[0:T, :]).then_inc(y_st, 1)
                dve.wait_ge(y_st, b + 1)
                dve.sem_inc(met_dve, 1)
                dve.bn_aggr(YMV[0:T, :], YST[0:T, :]).then_inc(y_mv, 1)
                dve.wait_ge(y_rs, b + 1)
                dve.tensor_scalar(Y[0:T, :], R0[0:T, :], YMV[0:T, 0:1], YRS[0:T, 0:1],
                                  ALU.subtract, ALU.mult).then_inc(y_n, 1)
                dve.wait_ge(y_n, b + 1)
                dve.tensor_tensor(Y[0:T, :], Y[0:T, :], G0[0:T, :], ALU.mult).then_inc(y_g, 1)
                dve.wait_ge(y_g, b + 1)
                dve.tensor_tensor(Y[0:T, :], Y[0:T, :], B0[0:T, :], ALU.add).then_inc(y_ok, 1)
                if more:
                    queries0_low(b + 1)
                    values0(b + 1)
                dve.wait_ge(q1_h, b + 1)
                dve.tensor_tensor(Q1l[:, :, :].rearrange("p c t -> p (c t)"), PJ[:, 0, 0:C * T],
                                  Q1h[:, :, :].bitcast(F32).rearrange("p c t -> p (c t)"), ALU.subtract)\
                    .then_inc(q1_l, 1)
                dve.wait_ge(mk1_b, b + 1)
                for k in range(32, NH + 3):
                    if k < NH:
                        shift(b, k)
                    if k >= 35 and (k - 3) % 2 == 1:
                        probs_out(b, k - 3)
                    if k == 49:
                        repeat_sums(b, 2)
                unit_sums(b, 2, C * T)
                unit_outputs(b, 2)
                dve.wait_ge(out1_mm, b + 1)
                wait_from(dve, ost, 16 * b)
                dve.scalar_tensor_tensor(out=OUT[0:T, :], in0=PJ[0:T, 1, :], scalar=GT[0:T, 1:2], in1=Y[0:T, :],
                                         op0=ALU.mult, op1=ALU.add).then_inc(fin, 1)

            dve.wait_ge(gate_t, 1)
            batch(0, True)
            with dve.Fori(1, NB - 1) as b:
                batch(b, True)
            batch(NB - 1, False)

        @block.scalar
        def _(act):
            def keys0_high(q):
                act.wait_ge(k0_mm, q + 1)
                act.activation(KHL[:, 0, :], PJ[:, 1, 0:SW], ACT.Identity, bias=BK0[:, 0:1]).then_inc(k0_h, 1)

            def queries0_high(q):
                act.wait_ge(q0_mm, q + 1)
                for g in range(GR):
                    act.activation(QHL[:, 0, g, :], PJ[:, 1, g * T:(g + 1) * T], ACT.Identity,
                                   bias=BQ0[:, g:g + 1]).then_inc(q0_h, 1)

            def exps(b, k):
                act.wait_ge(shifted, NH * b + k + 1)
                if k >= 3:
                    act.wait_ge(pt_mm, NH * b + k - 2)
                else:
                    wait_from(act, pt_mm, NH * b)
                act.activation(PR[0:T, k % 3, 0:S], SCO[0:T, k % 3, 0:S], ACT.Exp, bias=MN[0:T, k:k + 1],
                               scale=-1.0, accum_out=SM[0:T, k:k + 1]).then_inc(prob, 1)

            def probs_out(b, k):
                act.wait_ge(pt_mm, NH * b + k + 1)
                h = k // HALF
                if k % HALF == 0:
                    wait_from(act, pv, NHALF * b + h - 1)
                act.activation(PT[0:SP, h % 2, k % HALF, :], TP[0:SP, k % 2, 0:SC * T], ACT.Copy).then_inc(pt_even, 1)

            act.wait_ge(l_sm, 16 * 11)
            act.activation(GT[:, 1:2], GT[:, 0:1], ACT.Tanh).then_inc(gate_t, 1)
            act.wait_ge(l_q1, 16)
            act.activation(BQ0[:, :], BQ0[:, :], ACT.Copy, scale=SCALE0).then_inc(w_q0b, 1)
            act.activation(WQ0[:, :, :], WQ0[:, :, :], ACT.Copy, scale=SCALE0).then_inc(w_q0, 1)
            act.wait_ge(w_q0b, 1)
            keys0_high(0)
            queries0_high(0)

            def batch(b, more):
                for k in range(35):
                    if 1 <= k <= 32:
                        exps(b, k - 1)
                    if k >= 3 and (k - 3) % 2 == 0:
                        probs_out(b, k - 3)
                    if 1 <= k <= 4:
                        act.wait_ge(at_ev, 4 * b + k)
                        act.wait_ge(v0_mm, b + 1)
                        act.activation(TH[:, k - 1, 0:SC * SP], AT[:, k - 1, 0:SC * SP], ACT.Copy).then_inc(at_h, 1)
                    if k in (8, 12, 16, 20):
                        m = (k - 8) // 4
                        act.wait_ge(k1_mm, 4 * b + m + 1)
                        act.activation(K1h[:, m, :], PJ[:, m % 2, 0:SW], ACT.Copy).then_inc(k1_h, 1)
                    if k in (24, 28, 32):
                        s = (k - 24) // 4
                        act.wait_ge(v1_mm, 3 * b + s + 1)
                        act.activation(V1[0:SP, s, :], PJ[0:SP, s % 2, :], ACT.Copy).then_inc(v1_ev, 1)
                if more:
                    keys0_high(b + 1)
                    queries0_high(b + 1)
                act.wait_ge(yt_mm, b + 1)
                act.activation(YT[:, :, :].rearrange("p c t -> p (c t)"), PJ[:, 1, 0:C * T], ACT.Copy)\
                    .then_inc(yt_ev, 1)
                act.wait_ge(q1_mm, b + 1)
                act.activation(Q1h[:, :, :].rearrange("p c t -> p (c t)"), PJ[:, 0, 0:C * T], ACT.Copy)\
                    .then_inc(q1_h, 1)
                for k in range(32, NH + 3):
                    if 33 <= k <= NH:
                        exps(b, k - 1)
                    if k >= 35 and (k - 3) % 2 == 0:
                        probs_out(b, k - 3)

            batch(0, True)
            with act.Fori(1, NB - 1) as b:
                batch(b, True)
            batch(NB - 1, False)

        @block.gpsimd
        def _(pool):
            def split_ctx_low(q):
                pool.wait_ge(ct_h, q + 1)
                pool.tensor_tensor(TL[:, :, :], CT[:, :, :], TH[:, :, :].bitcast(F32), ALU.subtract)\
                    .then_inc(ct_l, 1)

            def ctx_rstd(q):
                pool.wait_ge(c_mv, 3 * q + 3)
                pool.sem_inc(met_pool, 1)
                pool.tensor_scalar(CVE[0:SP, :], CMV[0:SP, :, 1], EPS1, None, ALU.add).then_inc(c_ve, 1)
                pool.wait_ge(c_ve, q + 1)
                pool.tensor_tensor(CRS[0:SP, :], CVE[0:SP, :], mhalf[0:SP, :], ALU.pow).then_inc(c_rs, 1)

            pool.wait_ge(ident0, 1)
            pool.affine_select(out=ident[:, :], in_=ident[:, :], compare_op=ALU.is_equal, fill=0.0, base=0,
                               pattern=[[-1, P]], channel_multiplier=1).then_inc(ready, 1)
            split_ctx_low(0)
            ctx_rstd(0)

            def batch(b, more):
                for c in range(C):
                    pool.wait_ge(at_h, 4 * b + c + 1)
                    pool.tensor_tensor(TL[:, c, 0:SC * SP], AT[:, c, 0:SC * SP], TH[:, c, 0:SC * SP].bitcast(F32),
                                       ALU.subtract).then_inc(at_l, 1)
                pool.wait_ge(l_mk1, 16 * b + 16)
                wait_from(pool, shifted, NH * b)
                pool.sem_inc(met_pool, 1)
                pool.tensor_scalar(MK1[0:T, :], MU[0:T, :], -1.0, BIG, ALU.add, ALU.mult).then_inc(mk1_a, 1)
                pool.wait_ge(mk1_a, b + 1)
                pool.sem_inc(met_pool, 1)
                pool.tensor_scalar(MK1[0:T, :], MK1[0:T, :], BIG, None, ALU.mult).then_inc(mk1_b, 1)
                pool.wait_ge(l_xn, 16 * b + 16)
                pool.tensor_tensor(XN[0:T, :], XN[0:T, :], BO0[0:T, :], ALU.add).then_inc(xb, 1)
                if more:
                    ctx_rstd(b + 1)
                    split_ctx_low(b + 1)
                pool.wait_ge(y_mv, b + 1)
                pool.sem_inc(met_pool, 1)
                pool.tensor_scalar(YVE[0:T, :], YMV[0:T, 1:2], EPS0, None, ALU.add).then_inc(y_ve, 1)
                pool.wait_ge(y_ve, b + 1)
                pool.tensor_tensor(YRS[0:T, :], YVE[0:T, :], mhalf[0:T, 0:1], ALU.pow).then_inc(y_rs, 1)

            batch(0, True)
            with pool.Fori(1, NB - 1) as b:
                batch(b, True)
            batch(NB - 1, False)


def kernel(**inputs):
    import numpy as np
    import concourse.bacc as bacc
    from concourse.bass_utils import run_bass_kernel_spmd

    a = {k: np.asarray(v) for k, v in inputs.items()}
    D, C, KVH, HD, GR = 512, 4, 8, 16, 4

    def chunked(w):
        return w.reshape(C, 128, -1).transpose(1, 0, 2)

    wq0 = a["L0_xattn_Wq"].reshape(D, 2, 4, GR, HD).transpose(0, 3, 1, 4, 2).reshape(D, D)
    wk0 = a["L0_xattn_Wk"].reshape(D, 2, 4, HD).transpose(0, 1, 3, 2).reshape(D, KVH * HD)
    wo0 = a["L0_xattn_Wo"].reshape(2, 4, 2, 2, HD, D).transpose(1, 2, 4, 0, 3, 5).reshape(128, C, D)
    bq0 = a["L0_xattn_bq"].reshape(2, 4, GR, HD).transpose(0, 3, 1, 2).reshape(128, GR)
    bk0 = a["L0_xattn_bk"].reshape(2, 4, HD).transpose(0, 2, 1).reshape(128, 1)
    x, c = a["x"], a["ctx_2048"]
    arrays = {
        "x_rows": x,
        "x_cols": x.transpose(0, 2, 1).reshape(x.shape[0], C, 128, x.shape[1]).transpose(0, 2, 1, 3),
        "ctx_rows": c,
        "ctx_cols": c.transpose(0, 2, 1).reshape(c.shape[0], C, 128, c.shape[1]).transpose(0, 2, 1, 3),
        "mask0": a["mask_Bx1xSxS2_ff0"][:, 0],
        "mask1": a["mask_BxS2_bf1"],
        "wq0": chunked(wq0), "wk0": chunked(wk0), "wv0": chunked(a["L0_xattn_Wv"]), "wo0": wo0,
        "bq0": bq0, "bk0": bk0, "bv0": a["L0_xattn_bv"], "bo0": a["L0_xattn_bo"],
        "gamma0": a["L0_xattn_gamma"], "beta0": a["L0_xattn_beta"],
        "wq1": chunked(a["L1_xattn_Wq"].T), "wk1": chunked(a["L1_xattn_Wk"].T),
        "wv1": chunked(a["L1_xattn_Wv"].T), "wo1": chunked(a["L1_xattn_Wo"].T),
        "gamma1": a["L1_xattn_ln_gamma"].reshape(C, 128).T, "beta1": a["L1_xattn_ln_beta"].reshape(C, 128).T,
        "gate": a["L1_xattn_gate"],
    }
    arrays = {k: np.ascontiguousarray(v) for k, v in arrays.items()}
    nc = bacc.Bacc("TRN2", target_bir_lowering=False, num_devices=1)
    args = [nc.dram_tensor(k, v.shape, mybir.dt.from_np(v.dtype), kind="ExternalInput").ap() for k, v in arrays.items()]
    out = nc.dram_tensor("out", x.shape, mybir.dt.float32, kind="ExternalOutput").ap()
    two_layer_cross_attention(nc, *args, out)
    r = run_bass_kernel_spmd(nc, [arrays], core_ids=[0])
    return r.results[0]["out"]
```

```python
from contextlib import ExitStack

import concourse.bass as bass
from concourse import mybir

F32 = mybir.dt.float32
F32R = mybir.dt.float32r
U8 = mybir.dt.uint8
ALU = mybir.AluOpType
ACT = mybir.ActivationFunctionType

P = 128
BIG = 3.0e38


def wait_from(engine, semaphore, count):
    if not isinstance(count, int) or count > 0:
        engine.wait_ge(semaphore, count)


def two_layer_cross_attention(nc, x_rows, x_cols, ctx_rows, ctx_cols, mask0, mask1,
                              wq0, wk0, wv0, wo0, bq0, bk0, bv0, bo0, gamma0, beta0,
                              wq1, wk1, wv1, wo1, gamma1, beta1, gate, identity, repeat, out):
    NB, T, D = x_rows.shape
    S = ctx_rows.shape[1]
    C = D // P
    KVH, HD0 = 8, 16
    GR = D // (KVH * HD0)
    HD1 = 32
    SC = 3
    SP = -(-S // SC)
    SE = S + (S & 1)
    SW = 364
    NH = 48
    HALF = 8
    NHALF = NH // HALF
    NJ = 4
    ACT_OUTS, DVE_OUTS = 36, 12
    EPS0, EPS1 = 1e-6, 1e-5
    SCALE0, SCALE1 = HD0 ** -0.5, HD1 ** -0.5
    assert SC * SP <= SW and D == C * P and KVH * HD0 == P and SE <= 512

    with ExitStack() as ctx:
        def sb(name, shape, dt=F32):
            return ctx.enter_context(nc.sbuf_tensor(name, shape, dt))

        def sem(name):
            return ctx.enter_context(nc.semaphore(name))

        WQ0 = sb("WQ0", [P, C, D])
        WO0 = sb("WO0", [P, C, D])
        WQ1 = sb("WQ1", [P, C, D])
        WO1 = sb("WO1", [P, C, D])
        WK0h, WK0l = sb("WK0h", [P, C, P], F32R), sb("WK0l", [P, C, P], F32R)
        WV0h, WV0l = sb("WV0h", [P, C, P], F32R), sb("WV0l", [P, C, P], F32R)
        WK1h, WK1l = sb("WK1h", [P, C, D], F32R), sb("WK1l", [P, C, D], F32R)
        WV1h, WV1l = sb("WV1h", [P, C, D], F32R), sb("WV1l", [P, C, D], F32R)
        BQ0, BK0 = sb("BQ0", [P, GR]), sb("BK0", [P, 1])
        BV0 = sb("BV0", [P, P])
        BO0, G0, B0 = sb("BO0", [P, D]), sb("G0", [P, D]), sb("B0", [P, D])
        G1, B1 = sb("G1", [P, C]), sb("B1", [P, C])
        GT = sb("GT", [P, 2])
        ident = sb("ident", [P, P])
        mhalf = sb("mhalf", [P, SC])

        AT = sb("AT", [P, C, SW])
        TH, TL = sb("TH", [P, C, SW], F32R), sb("TL", [P, C, SW], F32R)
        NAT = sb("NAT", [P, SC, D])
        CST, CMV, CVE, CRS = sb("CST", [P, SC, 6]), sb("CMV", [P, SC, 2]), sb("CVE", [P, SC]), sb("CRS", [P, SC])
        K1HL = sb("K1HL", [P, 2, 2, SW], F32R)
        K1S = sb("K1S", [P, NJ, C, SW], F32R)
        V1 = sb("V1", [P, SC, D])
        KHL = sb("KHL", [P, 2, SW], F32R)
        K0S = sb("K0S", [P, 4, SW], F32R)
        V0P = sb("V0P", [P, SC, KVH, 3 * HD0])
        XT = sb("XT", [P, C, T])
        XN = sb("XN", [P, D])
        QHL = sb("QHL", [P, 2, GR, T], F32R)
        Q1S = sb("Q1S", [P, NJ, C, T], F32R)
        RP = sb("RP", [P, 2, P], F32R)
        Q0S = sb("Q0S", [P, 4, GR, T], F32R)
        MK0, MU, MK1 = sb("MK0", [P, S]), sb("MU", [P, S], U8), sb("MK1", [P, S])
        PR = sb("PR", [P, 3, SW])
        MN, SM = sb("MN", [P, NH]), sb("SM", [P, NH])
        PT = sb("PT", [P, 2, HALF, SC * T])
        V1_flat = V1[:, :, :].rearrange("p a b -> p (a b)")
        PT_flat = PT[:, :, :, :].rearrange("p a b c -> p (a b c)")
        RSM = sb("RSM", [P, 16])
        SX = sb("SX", [P, C, P])
        RI = SX[:, :, :].rearrange("p a b -> p (a b)")
        OT = sb("OT", [P, C, T])
        R0, Y = sb("R0", [P, D]), sb("Y", [P, D])
        YST, YMV, YVE, YRS = sb("YST", [P, 6]), sb("YMV", [P, 2]), sb("YVE", [P, 1]), sb("YRS", [P, 1])
        YT = sb("YT", [P, C, T])
        OUT = R0

        k_scr = nc.dram_tensor("k_scr", (2, 2, P // 2, SW), F32, kind="Internal").ap()
        k1_scr = nc.dram_tensor("k1_scr", (2, 2, P, 2 * SW), F32, kind="Internal").ap()
        q_scr = nc.dram_tensor("q_scr", (2, P, GR * T), F32, kind="Internal").ap()

        SCO = ctx.enter_context(nc.psum_tensor("SCO", [P, 3, 512], F32))
        TP = ctx.enter_context(nc.psum_tensor("TP", [P, 2, 512], F32))
        OA = ctx.enter_context(nc.psum_tensor("OA", [P, 512], F32))
        PJ = ctx.enter_context(nc.psum_tensor("PJ", [P, 2, 512], F32))

        l_w0, l_w1, l_q1, l_o, l_sm = sem("l_w0"), sem("l_w1"), sem("l_q1"), sem("l_o"), sem("l_sm")
        l_ct, l_nat, l_xt, l_xn = sem("l_ct"), sem("l_nat"), sem("l_xt"), sem("l_xn")
        l_mk0, l_mk1 = sem("l_mk0"), sem("l_mk1")
        kst, kld, qld = ([sem(f"{n}{par}") for par in range(2)] for n in ("kst", "kld", "qld"))
        k1st, k1ld = ([sem(f"{n}{half}") for half in range(2)] for n in ("k1st", "k1ld"))
        qst, ost, l_id = sem("qst"), sem("ost"), sem("l_id")
        rep_id, rep_mm, rep_act, rep_dve = sem("rep_id"), sem("rep_mm"), sem("rep_act"), sem("rep_dve")
        ct_l2 = sem("ct_l2")
        w_h, w_split, w_q0, ready = sem("w_h"), sem("w_split"), sem("w_q0"), sem("ready")
        gate_t, w_q0b, ready_parts, nat_zero = sem("gate_t"), sem("w_q0b"), sem("ready_parts"), sem("nat_zero")
        ident0 = sem("ident0")
        ct_h, ct_l = sem("ct_h"), sem("ct_l")
        k0_mm, k0_h, k0_l = sem("k0_mm"), sem("k0_h"), sem("k0_l")
        q0_mm, q0_h, q0_l = sem("q0_mm"), sem("q0_h"), sem("q0_l")
        v0_mm, v0_ev = sem("v0_mm"), sem("v0_ev")
        c_st, c_mv, c_ve, c_rs, c_nrm = sem("c_st"), sem("c_mv"), sem("c_ve"), sem("c_rs"), sem("c_nrm")
        at_mm, at_ev, at_h, at_l = sem("at_mm"), sem("at_ev"), sem("at_h"), sem("at_l")
        k1_mm, k1_h, k1_l = sem("k1_mm"), sem("k1_h"), sem("k1_l")
        v1_mm, v1_ev = sem("v1_mm"), sem("v1_ev")
        mk1_a, mk1_b = sem("mk1_a"), sem("mk1_b")
        scored, shifted, prob = sem("scored"), sem("shifted"), sem("prob")
        pt_mm, pt_act, pt_dve = sem("pt_mm"), sem("pt_act"), sem("pt_dve")
        rcp, sums_x = sem("rcp"), sem("sums_x")
        pv, sums_t, inv, attn = sem("pv"), sem("sums_t"), sem("inv"), sem("attn")
        xb, out0_mm, res, y_st, y_mv, y_ve, y_rs = (sem("xb"), sem("out0_mm"), sem("res"), sem("y_st"),
                                                    sem("y_mv"), sem("y_ve"), sem("y_rs"))
        y_n, y_ok, yt_mm, yt_ev = sem("y_n"), sem("y_ok"), sem("yt_mm"), sem("yt_ev")
        q1_mm, q1_h, q1_l, out1_mm, fin = sem("q1_mm"), sem("q1_h"), sem("q1_l"), sem("out1_mm"), sem("fin")

        met_dve, met_pool, met_sp = sem("met_dve"), sem("met_pool"), sem("met_sp")

        def spans(counts):
            ends = {}
            at = 0
            for k in sorted(counts):
                ends[k] = (at, at + counts[k])
                at += counts[k]
            return ends

        K1_STEPS = spans({7: 3, 8: 1, 9: 1, 10: 1, 13: 1, 14: 1, 15: 1, 16: 3, 17: 3, 18: 3, 19: 2, 20: 2, 21: 2,
                          22: 3, 23: 3, 24: 3, 25: 3, 26: 3, 27: 2, 28: 2, 29: 2, 30: 3})
        Q0_STEPS = spans({32: 4, 33: 3, 34: 3, 35: 2, 36: 2, 37: 2})
        K0_STEPS = spans({34: 1, 35: 2, 36: 3, 37: 3, 38: 3})
        V0_STEPS = spans({39: 1, 40: 2, 41: 2, 42: 2, 43: 2, 44: 2, 45: 1})
        K1_DONE = [max(k for k, (i, _) in K1_STEPS.items() if i < 12 * (m + 1)) for m in range(C)]
        REP_BANK = (SCO[:, 2, 0:C * T], TP[:, 0, 0:C * T], TP[:, 1, 0:C * T], SCO[:, 0, 0:C * T])

        def copied_out(b, k):
            if k % 4 == 1:
                return pt_dve, DVE_OUTS * b + (k + 3) // 4
            return pt_act, ACT_OUTS * b + k + 1 - (k + 3) // 4

        block = ctx.enter_context(nc.Block())

        @block.sync
        def _(sp):
            def load_ctx_cols(q):
                sp.dma_start(AT[:, :, 0:S], ctx_cols[q]).then_inc(l_ct, 16)

            def load_ctx_rows(q):
                full = (SC - 1) * SP
                sp.dma_start(NAT[0:SP, 0:SC - 1, :],
                             ctx_rows[q, 0:full, :].rearrange("(c p) d -> p c d", p=SP)).then_inc(l_nat, 16)
                sp.dma_start(NAT[0:S - full, SC - 1, :], ctx_rows[q, full:S, :]).then_inc(l_nat, 16)

            def spread_heads0(q):
                def store_keys(par):
                    for hl in range(2):
                        sp.dma_start(k_scr[par, hl], KHL[64 * par:64 * par + 64, hl, :].bitcast(F32))\
                            .then_inc(kst[par], 16)

                def load_keys(par):
                    sp.wait_ge(kst[par], 32 * q + 32)
                    src = k_scr[par].rearrange("a (d i) s -> (a d) i s", i=4)
                    for e in range(2):
                        at = 64 * par + 32 * e
                        sp.dma_start(K0S[at:at + 32, :, :].bitcast(F32), src).then_inc(kld[par], 16)

                def load_queries(par):
                    for hl in range(2):
                        for e in range(2):
                            at = 64 * par + 32 * hl + 16 * e
                            src = q_scr[hl, 64 * par:64 * par + 64, :].rearrange("(d i) s -> d i s", i=4)
                            dst = Q0S[at:at + 16, :, :, :].bitcast(F32).rearrange("d i g t -> d i (g t)")
                            sp.dma_start(dst, src).then_inc(qld[par], 16)

                sp.wait_ge(q0_h, 4 * q + 4)
                sp.wait_ge(q0_l, 4 * q + 4)
                for hl in range(2):
                    sp.dma_start(q_scr[hl], QHL[:, hl, :, :].bitcast(F32)).then_inc(qst, 16)
                sp.wait_ge(k0_h, q + 1)
                sp.wait_ge(k0_l, q + 1)
                store_keys(0)
                sp.wait_ge(qst, 32 * q + 32)
                load_queries(0)
                load_keys(0)
                store_keys(1)
                load_queries(1)
                load_keys(1)

            def spread_keys1(b, half):
                sp.wait_ge(k1_h, 4 * b + 2 * half + 2)
                sp.wait_ge(k1_l, 4 * b + 2 * half + 2)
                for hl in range(2):
                    sp.dma_start(k1_scr[hl, half], K1HL[:, hl, :, :].bitcast(F32).rearrange("p m s -> p (m s)"))\
                        .then_inc(k1st[half], 16)
                sp.wait_ge(k1st[half], 32 * b + 32)
                for term in range(4):
                    src = k1_scr[term % 2, half].rearrange("(j d) f -> d j f", d=HD1)
                    dst = K1S[32 * term:32 * term + 32, :, 2 * half:2 * half + 2, :].bitcast(F32)
                    sp.dma_start(dst.rearrange("d j m s -> d j (m s)"), src).then_inc(k1ld[half], 16)

            sp.dma_start(AT[:, :, 0:S], ctx_cols[0]).then_inc(l_ct, 16)
            for n, w in enumerate((wk0, wv0)):
                sp.dma_start(V1_flat[:, n * C * P:(n + 1) * C * P], w.rearrange("p c n -> p (c n)")).then_inc(l_w0, 16)
            sp.dma_start(XT[:, :, :], x_cols[0]).then_inc(l_xt, 16)
            sp.dma_start(ident[:, :], identity).then_inc(l_id, 16)
            sp.dma_start(SX[:, 0:2, :], repeat).then_inc(l_id, 16)
            sp.dma_start(WQ0[:, :, :], wq0).then_inc(l_q1, 16)
            for dst, src in ((BQ0, bq0), (BK0, bk0), (G1, gamma1), (B1, beta1)):
                sp.dma_start(dst[:, :], src).then_inc(l_sm, 16)
            for dst, src in ((BV0, bv0), (BO0, bo0), (G0, gamma0), (B0, beta0)):
                sp.dma_start(dst[:, :], src.partition_broadcast(P)).then_inc(l_sm, 16)
            sp.dma_start(GT[:, 0:1], gate.partition_broadcast(P)).then_inc(l_sm, 16)
            sp.wait_ge(nat_zero, 1)
            load_ctx_rows(0)
            for n, w in enumerate((wk1, wv1)):
                sp.dma_start(PT_flat[:, n * C * D:(n + 1) * C * D], w.rearrange("p c n -> p (c n)")).then_inc(l_w1, 16)
            sp.dma_start(MK0[0:T, :], mask0[0]).then_inc(l_mk0, 16)
            sp.dma_start(MU[0:T, :], mask1[0].partition_broadcast(T)).then_inc(l_mk1, 16)
            sp.dma_start(XN[0:T, :], x_rows[0]).then_inc(l_xn, 16)
            sp.dma_start(WO0[:, :, :], wo0).then_inc(l_o, 16)
            sp.dma_start(WQ1[:, :, :], wq1).then_inc(l_o, 16)
            sp.dma_start(WO1[:, :, :], wo1).then_inc(l_o, 16)
            spread_heads0(0)

            def batch(b, first):
                sp.wait_ge(at_mm, 4 * b + 4)
                load_ctx_rows(b + 1)
                sp.wait_ge(mk1_a, b + 1)
                sp.sem_inc(met_sp, 1)
                sp.dma_start(MU[0:T, :], mask1[b + 1].partition_broadcast(T)).then_inc(l_mk1, 16)
                if not first:
                    sp.wait_ge(fin, b)
                    sp.dma_start(out[b - 1], OUT[0:T, :]).then_inc(ost, 16)
                sp.wait_ge(at_h, 4 * b + 4)
                sp.wait_ge(at_l, 4 * b + 4)
                load_ctx_cols(b + 1)
                sp.wait_ge(q0_mm, b + 1)
                sp.dma_start(XT[:, :, :], x_cols[b + 1]).then_inc(l_xt, 16)
                spread_keys1(b, 0)
                spread_keys1(b, 1)
                sp.wait_ge(shifted, NH * b + 32)
                sp.dma_start(MK0[0:T, :], mask0[b + 1]).then_inc(l_mk0, 16)
                sp.wait_ge(res, b + 1)
                sp.dma_start(XN[0:T, :], x_rows[b + 1]).then_inc(l_xn, 16)
                spread_heads0(b + 1)

            batch(0, True)
            with sp.Fori(1, NB - 1) as b:
                batch(b, False)
            for n in (NB - 2, NB - 1):
                sp.wait_ge(fin, n + 1)
                sp.dma_start(out[n], OUT[0:T, :]).then_inc(ost, 16)
                if n == NB - 2:
                    spread_keys1(NB - 1, 0)
                    spread_keys1(NB - 1, 1)
            sp.wait_ge(ost, 16 * NB)

        @block.tensor
        def _(pe):
            def mm3(dst, wh, wl, xh, xl, start, stop):
                pe.matmul(dst, wh, xh, start=start, stop=False)
                pe.matmul(dst, wl, xh, start=False, stop=False)
                return pe.matmul(dst, wh, xl, start=False, stop=stop)

            def mm3_step(term, dst, wh, wl, xh, xl, start, stop):
                w, x = ((wh, xh), (wl, xh), (wh, xl))[term]
                return pe.matmul(dst, w, x, start=start and term == 0, stop=stop and term == 2)

            def keys0(steps=range(3 * C)):
                for i in steps:
                    c, term = divmod(i, 3)
                    last = mm3_step(term, PJ[:, 1, 0:SW], WK0h[:, c, :], WK0l[:, c, :], TH[:, c, :], TL[:, c, :],
                                    c == 0, c == C - 1)
                    if i == 3 * C - 1:
                        last.then_inc(k0_mm, 1)

            def queries0(steps=range(GR * C)):
                for i in steps:
                    g, c = divmod(i, C)
                    last = pe.matmul(PJ[:, 0, g * T:(g + 1) * T], WQ0[:, c, g * P:(g + 1) * P],
                                     XT[:, c, :], start=c == 0, stop=c == C - 1)
                    if i == GR * C - 1:
                        last.then_inc(q0_mm, 1)

            def values0(steps=range(SC * C)):
                for i in steps:
                    s, c = divmod(i, C)
                    rows = slice(s * SP, (s + 1) * SP)
                    last = mm3(PJ[0:SP, 0, s * P:(s + 1) * P], TH[:, c, rows], TL[:, c, rows],
                               WV0h[:, c, :], WV0l[:, c, :], c == 0, c == C - 1)
                    if i == SC * C - 1:
                        last.then_inc(v0_mm, 1)

            def score(b, k):
                dst = SCO[0:T, k % 3, 0:SE]
                if k < 32:
                    G, gh, gl, j = k // 16, k // 8 % 2, k // 4 % 2, k % 4
                    pe.matmul(dst, Q0S[64 * G:64 * G + 64, j, 2 * gh + gl, :], K0S[64 * G:64 * G + 64, j, 0:SE],
                              start=True, stop=True).then_inc(scored, 1)
                else:
                    m, j = (k - 32) // 4, k % 4
                    pe.matmul(dst, Q1S[:, j, m, :], K1S[:, j, m, 0:SE], start=True, stop=True).then_inc(scored, 1)

            def transpose_probs(b, k):
                pe.wait_ge(prob, NH * b + k + 1)
                for c in range(SC):
                    last = pe.transpose(TP[0:SP, k % 2, c * T:(c + 1) * T], PR[0:T, k % 3, c * SP:(c + 1) * SP],
                                        ident[0:T, 0:T])
                last.then_inc(pt_mm, 1)

            def free_tp(b, k):
                if k >= 2:
                    pe.wait_ge(*copied_out(b, k - 2))
                elif not isinstance(b, int) or b > 0:
                    pe.wait_ge(*copied_out(b - 1, k - 2 + NH))

            def out_half(b, h, parts):
                for part in parts:
                    ml, c = divmod(part, SC)
                    if part == 0:
                        pe.wait_ge(pt_act, ACT_OUTS * b + 6 * h + 6)
                        pe.wait_ge(pt_dve, DVE_OUTS * b + 2 * h + 2)
                        if h % 2 == 0:
                            wait_from(pe, attn, 3 * b + h // 2)
                    for j in range(NJ):
                        if h < 4:
                            G, gh = h // 2, h % 2
                            lhs = V0P[0:SP, c, 4 * G + j, (HD0, 0)[gh]:(HD0, 0)[gh] + 32]
                            rhs = PT[0:SP, h % 2, :, c * T:(c + 1) * T].rearrange("p (a j) t -> p a j t", j=NJ)[:, :, j, :]
                            last = pe.matmul(OA[32 * j:32 * j + 32, 0:2 * T], lhs, rhs,
                                             start=gh == 0 and c == 0, stop=gh == 1 and c == SC - 1)
                        else:
                            m = 2 * (h - 4) + ml
                            head = 4 * m + j
                            last = pe.matmul(OA[32 * j:32 * j + 32, m * T:(m + 1) * T],
                                             V1[0:SP, c, head * HD1:(head + 1) * HD1],
                                             PT[0:SP, h % 2, 4 * ml + j, c * T:(c + 1) * T],
                                             start=c == 0, stop=c == SC - 1)
                    if part == (2 if h < 4 else 5):
                        last.then_inc(pv, 1)

            def sums_transposed(b, u):
                dst = OA[:, 2 * T:4 * T] if u < 2 else PJ[:, 0, :]
                pe.wait_ge(sums_x, 3 * b + u + 1)
                for m in range(2 if u < 2 else C):
                    last = pe.transpose(dst[:, m * T:(m + 1) * T], SX[0:T, m, :], ident[0:T, 0:T])
                last.then_inc(sums_t, 1)

            def out0(b):
                for c in range(C):
                    last = pe.matmul(PJ[0:T, 0, :], OT[:, c, :], WO0[:, c, :], start=c == 0, stop=c == C - 1)
                last.then_inc(out0_mm, 1)

            def out1(b, steps):
                for i in steps:
                    half, c = divmod(i, C)
                    cols = slice(half * (D // 2), (half + 1) * (D // 2))
                    last = pe.matmul(PJ[0:T, 1, cols], OT[:, c, :], WO1[:, c, cols], start=c == 0, stop=c == C - 1)
                    if i == 2 * C - 1:
                        last.then_inc(out1_mm, 1)

            def ctx_transposed(b, c):
                for s in range(SC):
                    last = pe.transpose(PJ[:, c % 2, s * SP:(s + 1) * SP], NAT[0:SP, s, c * P:(c + 1) * P],
                                        ident[0:SP, 0:SP])
                last.then_inc(at_mm, 1)

            def keys1(b, i):
                m, c, term = i // (3 * C), i // 3 % C, i % 3
                cols = slice(m * P, (m + 1) * P)
                last = mm3_step(term, PJ[:, m % 2, 0:SW], WK1h[:, c, cols], WK1l[:, c, cols], TH[:, c, :],
                                TL[:, c, :], c == 0, c == C - 1)
                if i % (3 * C) == 3 * C - 1:
                    last.then_inc(k1_mm, 1)

            V1_BANK = (PJ[0:SP, 1, :], SCO[0:SP, 0, :], SCO[0:SP, 1, :])

            def values1(b, steps):
                for i in steps:
                    s, c = divmod(i, C)
                    rows = slice(s * SP, (s + 1) * SP)
                    last = mm3(V1_BANK[s], TH[:, c, rows], TL[:, c, rows], WV1h[:, c, :], WV1l[:, c, :],
                               c == 0, c == C - 1)
                    if c == C - 1:
                        last.then_inc(v1_mm, 1)

            pe.wait_ge(l_id, 32)
            pe.wait_ge(ready_parts, 4)
            pe.wait_ge(w_split, 2)
            pe.wait_ge(ct_h, 1)
            pe.wait_ge(ct_l, 1)
            pe.wait_ge(ct_l2, 1)
            keys0()
            pe.wait_ge(w_q0, 1)
            pe.wait_ge(l_xt, 16)
            queries0()
            pe.wait_ge(q0_l, 4)
            values0()
            pe.wait_ge(w_split, 4)
            pe.wait_ge(l_o, 48)

            def batch(b, first, more):
                for k in range(34):
                    if k < 32:
                        if k % 16 == 0:
                            pe.wait_ge(kld[k // 16], 32 * b + 32)
                            pe.wait_ge(qld[k // 16], 64 * b + 64)
                        if k >= 3 or not first:
                            pe.wait_ge(prob, NH * b + k - 2)
                        score(b, k)
                    if k in (0, 2, 4, 6):
                        c = k // 2
                        if c == 0:
                            pe.wait_ge(c_nrm, 3 * b + 3)
                            pe.wait_ge(v0_ev, b + 1)
                        elif c == 1:
                            pe.wait_ge(k0_l, b + 1)
                        else:
                            pe.wait_ge(at_ev, 4 * b + c - 1)
                        ctx_transposed(b, c)
                    if k < 2 and not first:
                        free_tp(b - 1, NH - 2 + k)
                        transpose_probs(b - 1, NH - 2 + k)
                    if k >= 2:
                        free_tp(b, k - 2)
                        transpose_probs(b, k - 2)
                    if k in (3, 4, 5) and not first:
                        out_half(b - 1, 5, range(2 * (k - 3), 2 * (k - 3) + 2))
                        if k == 5:
                            pe.wait_ge(at_ev, 4 * b + 3)
                            sums_transposed(b - 1, 2)
                    if 8 <= k < 16 and not first:
                        if k == 8:
                            pe.wait_ge(attn, 3 * b)
                            pe.wait_ge(at_ev, 4 * b + 4)
                        out1(b - 1, range(k - 8, k - 7))
                    for i in range(*K1_STEPS.get(k, (0, 0))):
                        if i < 3 * C and i % 3 == 0:
                            pe.wait_ge(at_h, 4 * b + i // 3 + 1)
                            pe.wait_ge(at_l, 4 * b + i // 3 + 1)
                        if i == 0:
                            pe.wait_ge(at_ev, 4 * b + 3)
                            if not first:
                                pe.wait_ge(inv, 3 * b)
                        elif i == 3 * C:
                            pe.wait_ge(at_ev, 4 * b + 4)
                            if not first:
                                pe.wait_ge(fin, b)
                        elif i % (3 * C) == 0:
                            pe.wait_ge(k1_l, 4 * b + i // (3 * C) - 1)
                        keys1(b, i)
                    if k in (11, 12, 13, 19, 20, 21, 27, 28, 29):
                        out_half(b, (k - 11) // 8, range((k - 11) % 8, (k - 11) % 8 + 1))
                    if k == 21:
                        sums_transposed(b, 0)
                    if k in (32, 33):
                        if k == 32:
                            pe.wait_ge(k1_l, 4 * b + 4)
                        values1(b, range(k - 32, k - 31))
                out_half(b, 3, range(3))
                sums_transposed(b, 1)
                values1(b, range(2, 4))
                pe.wait_ge(k1_l, 4 * b + 3)
                pe.wait_ge(attn, 3 * b + 2)
                out0(b)
                pe.wait_ge(prob, NH * b + 31)
                values1(b, range(4, 8))
                pe.wait_ge(prob, NH * b + 32)
                values1(b, range(8, 9))
                pe.wait_ge(y_ok, b + 1)
                for c in range(C):
                    last = pe.transpose(PJ[:, 0, c * T:(c + 1) * T], Y[0:T, c * P:(c + 1) * P], ident[0:T, 0:T])
                last.then_inc(yt_mm, 1)
                values1(b, range(9, 10))
                pe.wait_ge(v1_ev, 3 * b + 1)
                pe.wait_ge(yt_ev, b + 1)
                for m in range(C):
                    for c in range(C):
                        last = pe.matmul(PJ[:, 1, m * T:(m + 1) * T], WQ1[:, c, m * P:(m + 1) * P], YT[:, c, :],
                                         start=c == 0, stop=c == C - 1)
                last.then_inc(q1_mm, 1)
                values1(b, range(10, 12))
                pe.wait_ge(v1_ev, 3 * b + 2)
                pe.wait_ge(q1_h, b + 1)
                pe.wait_ge(q1_l, b + 1)
                for j in range(NJ):
                    r = slice(32 * j, 32 * j + 32)
                    for hl in range(2):
                        last = pe.matmul(REP_BANK[j], RP[r, hl, :], QHL[r, hl, :, :].rearrange("p m t -> p (m t)"),
                                         start=hl == 0, stop=hl == 1)
                    last.then_inc(rep_mm, 1)
                if more:
                    pe.wait_ge(l_xt, 16 * b + 32)
                for k in range(32, NH):
                    if more and k in Q0_STEPS:
                        queries0(range(*Q0_STEPS[k]))
                    if k == 32:
                        pe.wait_ge(rep_act, 2 * b + 2)
                        pe.wait_ge(rep_dve, 2 * b + 2)
                        pe.wait_ge(k1ld[0], 64 * b + 64)
                    if k == 34:
                        pe.wait_ge(v1_ev, 3 * b + 3)
                    if k == 40:
                        pe.wait_ge(k1ld[1], 64 * b + 64)
                    if k >= 35:
                        pe.wait_ge(prob, NH * b + k - 2)
                    score(b, k)
                    if more and k in K0_STEPS:
                        if k == 34:
                            pe.wait_ge(ct_h, b + 2)
                            pe.wait_ge(ct_l2, b + 2)
                        elif k == 36:
                            pe.wait_ge(ct_l, b + 2)
                        keys0(range(*K0_STEPS[k]))
                    if more and k in V0_STEPS:
                        if k == 39:
                            pe.wait_ge(q0_l, 4 * b + 8)
                        values0(range(*V0_STEPS[k]))
                    if k >= 34:
                        free_tp(b, k - 2)
                        transpose_probs(b, k - 2)
                    if k >= 43:
                        out_half(b, 4, range(k - 43, k - 42) if k < 47 else range(4, 6))

            batch(0, True, True)
            with pe.Fori(1, NB - 1) as b:
                batch(b, False, True)
            batch(NB - 1, False, False)
            for k in (NH - 2, NH - 1):
                free_tp(NB - 1, k)
                transpose_probs(NB - 1, k)
            out_half(NB - 1, 5, range(6))
            sums_transposed(NB - 1, 2)
            pe.wait_ge(attn, 3 * NB)
            out1(NB - 1, range(2 * C))

        @block.vector
        def _(dve):
            def split_ctx(q):
                dve.wait_ge(l_ct, 16 * q + 16)
                dve.tensor_copy(TH[:, :, :], AT[:, :, :]).then_inc(ct_h, 1)
                dve.wait_ge(ct_h, q + 1)
                dve.tensor_tensor(TL[:, 0:2, :], AT[:, 0:2, :], TH[:, 0:2, :].bitcast(F32), ALU.subtract)\
                    .then_inc(ct_l2, 1)

            def keys0_low(q):
                dve.wait_ge(k0_h, q + 1)
                dve.scalar_tensor_tensor(out=KHL[:, 1, :], in0=PJ[:, 1, 0:SW], scalar=BK0[:, 0:1],
                                         in1=KHL[:, 0, :].bitcast(F32), op0=ALU.add, op1=ALU.subtract)\
                    .then_inc(k0_l, 1)

            def queries0_low(q):
                for g in range(GR):
                    dve.wait_ge(q0_h, 4 * q + 4)
                    dve.scalar_tensor_tensor(out=QHL[:, 1, g, :], in0=PJ[:, 0, g * T:(g + 1) * T],
                                             scalar=BQ0[:, g:g + 1], in1=QHL[:, 0, g, :].bitcast(F32),
                                             op0=ALU.add, op1=ALU.subtract).then_inc(q0_l, 1)

            def values0(q):
                dve.wait_ge(v0_mm, q + 1)
                dve.tensor_tensor(V0P[0:SP, :, :, HD0:2 * HD0],
                                  PJ[0:SP, 0, 0:SC * P].rearrange("p (s h d) -> p s h d", s=SC, h=KVH),
                                  BV0[0:SP, :].rearrange("p (h d) -> p h d", h=KVH).unsqueeze(1)
                                  .to_broadcast([SP, SC, KVH, HD0]), ALU.add)\
                    .then_inc(v0_ev, 1)

            def ctx_stats(q, s):
                if s == 0:
                    dve.wait_ge(l_nat, 32 * q + 32)
                dve.bn_stats(CST[0:SP, s, :], NAT[0:SP, s, :]).then_inc(c_st, 1)

            def ctx_mean(q):
                dve.wait_ge(c_st, 3 * q + 3)
                dve.sem_inc(met_dve, 1)
                for s in range(SC):
                    dve.bn_aggr(CMV[0:SP, s, :], CST[0:SP, s, :]).then_inc(c_mv, 1)

            def ctx_normalise(q, s):
                dve.wait_ge(c_rs, q + 1)
                dve.tensor_scalar(NAT[0:SP, s, :], NAT[0:SP, s, :], CMV[0:SP, s, 0:1], CRS[0:SP, s:s + 1],
                                  ALU.subtract, ALU.mult).then_inc(c_nrm, 1)

            def shift(b, k):
                dve.wait_ge(scored, NH * b + k + 1)
                dve.sem_inc(met_dve, 1)
                bank = SCO[0:T, k % 3, 0:S]
                mask, scale = (MK0, -1.0) if k < 32 else (MK1, -SCALE1)
                dve.tensor_tensor_reduce(out=bank, in0=bank, in1=mask[0:T, :], scale=scale, scalar=3.4e38,
                                         op0=ALU.add, op1=ALU.min, accum_out=MN[0:T, k:k + 1]).then_inc(shifted, 1)

            def probs_out(b, k):
                dve.wait_ge(pt_mm, NH * b + k + 1)
                h = k // HALF
                if k % HALF == 1:
                    wait_from(dve, pv, NHALF * b + h - 1)
                dve.tensor_copy(PT[0:SP, h % 2, k % HALF, :], TP[0:SP, k % 2, 0:SC * T]).then_inc(pt_dve, 1)

            def repeat_sums(b, u):
                dve.wait_ge(prob, NH * b + 16 * u + 16)
                wait_from(dve, sums_x, 3 * b + u)
                dve.reciprocal(RSM[0:T, :], SM[0:T, 16 * u:16 * u + 16]).then_inc(rcp, 1)
                wait_from(dve, attn, 3 * b + u)
                dve.wait_ge(rcp, 3 * b + u + 1)
                sums = RSM[0:T, :]
                if u < 2:
                    src = sums.rearrange("p (a g j) -> p g j a", a=2, g=2).unsqueeze(4).to_broadcast([T, 2, NJ, 2, HD0])
                    dve.tensor_copy(SX[0:T, 0:2, :].rearrange("p g (j a d) -> p g j a d", j=NJ, a=2), src)\
                        .then_inc(sums_x, 1)
                else:
                    src = sums.unsqueeze(2).to_broadcast([T, 16, HD1])
                    dve.tensor_copy(SX[0:T, :, :].rearrange("p m (j d) -> p (m j) d", j=NJ), src).then_inc(sums_x, 1)

            def unit_outputs(b, u):
                dve.wait_ge(pv, NHALF * b + 2 * u + 2)
                dve.wait_ge(inv, 3 * b + u + 1)
                n = 2 * T if u < 2 else C * T
                dst = OT[:, 2 * u:2 * u + 2, :] if u < 2 else OT[:, :, :]
                dve.tensor_tensor(dst.rearrange("p c t -> p (c t)"), OA[:, 0:n], RI[:, 0:n], ALU.mult)\
                    .then_inc(attn, 1)

            def result(b):
                dve.wait_ge(out1_mm, b + 1)
                dve.scalar_tensor_tensor(out=OUT[0:T, :], in0=PJ[0:T, 1, :], scalar=GT[0:T, 1:2], in1=Y[0:T, :],
                                         op0=ALU.mult, op1=ALU.add).then_inc(fin, 1)

            dve.memset(AT[:, :, S:SW], 0.0).then_inc(ready_parts, 1)
            dve.memset(NAT[:, :, :], 0.0).then_inc(nat_zero, 1)
            dve.memset(V0P[:, :, :, :], 0.0).then_inc(ready_parts, 1)
            dve.memset(PR[:, :, :], 0.0).then_inc(ready_parts, 1)
            dve.memset(mhalf[:, :], -0.5).then_inc(ready_parts, 1)
            dve.wait_ge(l_id, 32)
            dve.tensor_copy(RP[:, :, :], SX[:, 0:2, :]).then_inc(rep_id, 1)
            dve.wait_ge(ready_parts, 4)
            dve.wait_ge(l_w0, 32)
            first = ((WK0h, WK0l), (WV0h, WV0l))
            for n, (wh, _) in enumerate(first):
                dve.tensor_copy(wh[:, :, :].rearrange("p c n -> p (c n)"), V1_flat[:, n * C * P:(n + 1) * C * P])\
                    .then_inc(w_h, 1)
            split_ctx(0)
            dve.wait_ge(w_h, 2)
            for n, (wh, wl) in enumerate(first):
                dve.tensor_tensor(wl[:, :, :].rearrange("p c n -> p (c n)"), V1_flat[:, n * C * P:(n + 1) * C * P],
                                  wh[:, :, :].bitcast(F32).rearrange("p c n -> p (c n)"), ALU.subtract)\
                    .then_inc(w_split, 1)
            dve.wait_ge(l_sm, 16 * 9)
            dve.wait_ge(k0_mm, 1)
            keys0_low(0)
            queries0_low(0)
            values0(0)
            for s in range(SC):
                ctx_stats(0, s)
            ctx_mean(0)
            dve.wait_ge(l_w1, 32)
            for n, (wh, wl) in enumerate(((WK1h, WK1l), (WV1h, WV1l))):
                part = PT_flat[:, n * C * D:(n + 1) * C * D]
                dve.tensor_copy(wh[:, :, :].rearrange("p c n -> p (c n)"), part).then_inc(w_h, 1)
                dve.wait_ge(w_h, 3 + n)
                dve.tensor_tensor(wl[:, :, :].rearrange("p c n -> p (c n)"), part,
                                  wh[:, :, :].bitcast(F32).rearrange("p c n -> p (c n)"), ALU.subtract)\
                    .then_inc(w_split, 1)
            for s in range(SC):
                ctx_normalise(0, s)
            dve.wait_ge(w_split, 4)

            def batch(b, first, more):
                dve.wait_ge(l_mk0, 16 * b + 16)
                for k in range(35):
                    if k < 32:
                        shift(b, k)
                    if k == 0 and not first:
                        probs_out(b - 1, NH - 3)
                    if 3 <= k and (k - 3) % 4 == 1:
                        probs_out(b, k - 3)
                    if k == 1 and not first:
                        repeat_sums(b - 1, 2)
                    if k in (0, 2, 4, 6):
                        c = k // 2
                        if c == 0:
                            dve.wait_ge(ct_l, b + 1)
                            dve.wait_ge(ct_l2, b + 1)
                        dve.wait_ge(at_mm, 4 * b + c + 1)
                        dve.tensor_scalar(AT[:, c, 0:SC * SP], PJ[:, c % 2, 0:SC * SP], G1[:, c:c + 1], B1[:, c:c + 1],
                                          ALU.mult, ALU.add).then_inc(at_ev, 1)
                    if k == 7 and not first:
                        unit_outputs(b - 1, 2)
                    if k == 16 and not first:
                        result(b - 1)
                    if k - 2 in K1_DONE:
                        m = K1_DONE.index(k - 2)
                        dve.wait_ge(k1_h, 4 * b + m + 1)
                        dve.tensor_tensor(K1HL[:, 1, m % 2, :], PJ[:, m % 2, 0:SW], K1HL[:, 0, m % 2, :].bitcast(F32),
                                          ALU.subtract).then_inc(k1_l, 1)
                    if k == 18:
                        repeat_sums(b, 0)
                    if k == 23:
                        unit_outputs(b, 0)
                    if more and k in (14, 16, 20):
                        ctx_stats(b + 1, (14, 16, 20).index(k))
                    if more and k == 24:
                        ctx_mean(b + 1)
                    if more and k in (28, 29, 30):
                        ctx_normalise(b + 1, k - 28)
                    if k == 33:
                        repeat_sums(b, 1)
                unit_outputs(b, 1)
                dve.wait_ge(out0_mm, b + 1)
                dve.wait_ge(xb, b + 1)
                if not first:
                    dve.wait_ge(ost, 16 * b)
                dve.tensor_tensor(R0[0:T, :], PJ[0:T, 0, :], XN[0:T, :], ALU.add).then_inc(res, 1)
                dve.wait_ge(res, b + 1)
                dve.bn_stats(YST[0:T, :], R0[0:T, :]).then_inc(y_st, 1)
                dve.wait_ge(y_st, b + 1)
                dve.sem_inc(met_dve, 1)
                dve.bn_aggr(YMV[0:T, :], YST[0:T, :]).then_inc(y_mv, 1)
                dve.wait_ge(y_mv, b + 1)
                dve.scalar_tensor_tensor(out=Y[0:T, :], in0=R0[0:T, :], scalar=YMV[0:T, 0:1], in1=G0[0:T, :],
                                         op0=ALU.subtract, op1=ALU.mult).then_inc(y_n, 1)
                dve.wait_ge(y_n, b + 1)
                dve.wait_ge(y_rs, b + 1)
                dve.scalar_tensor_tensor(out=Y[0:T, :], in0=Y[0:T, :], scalar=YRS[0:T, 0:1], in1=B0[0:T, :],
                                         op0=ALU.mult, op1=ALU.add).then_inc(y_ok, 1)
                dve.wait_ge(q1_h, b + 1)
                dve.tensor_tensor(QHL[:, 1, :, :].rearrange("p m t -> p (m t)"), PJ[:, 1, 0:C * T],
                                  QHL[:, 0, :, :].bitcast(F32).rearrange("p m t -> p (m t)"), ALU.subtract)\
                    .then_inc(q1_l, 1)
                for j in (1, 3):
                    dve.wait_ge(rep_mm, 4 * b + j + 1)
                    dve.tensor_copy(Q1S[:, j, :, :].rearrange("p m t -> p (m t)"), REP_BANK[j]).then_inc(rep_dve, 1)
                dve.wait_ge(mk1_b, b + 1)
                for k in range(32, NH):
                    shift(b, k)
                    if k == 32 and more:
                        dve.wait_ge(v1_mm, 3 * b + 3)
                        split_ctx(b + 1)
                    if k >= 35 and (k - 3) % 4 == 1:
                        probs_out(b, k - 3)
                    if more and k == 38:
                        queries0_low(b + 1)
                    if more and k == 41:
                        keys0_low(b + 1)
                    if more and k == 44:
                        values0(b + 1)

            dve.wait_ge(gate_t, 1)
            batch(0, True, True)
            with dve.Fori(1, NB - 1) as b:
                batch(b, False, True)
            batch(NB - 1, False, False)
            probs_out(NB - 1, NH - 3)
            repeat_sums(NB - 1, 2)
            unit_outputs(NB - 1, 2)
            result(NB - 1)

        @block.scalar
        def _(act):
            def keys0_high(q):
                act.wait_ge(k0_mm, q + 1)
                act.activation(KHL[:, 0, :], PJ[:, 1, 0:SW], ACT.Identity, bias=BK0[:, 0:1]).then_inc(k0_h, 1)

            def queries0_high(q):
                act.wait_ge(q0_mm, q + 1)
                wait_from(act, rep_mm, 4 * q)
                for g in range(GR):
                    act.activation(QHL[:, 0, g, :], PJ[:, 0, g * T:(g + 1) * T], ACT.Identity,
                                   bias=BQ0[:, g:g + 1]).then_inc(q0_h, 1)

            def exps(b, k):
                act.wait_ge(shifted, NH * b + k + 1)
                if k >= 3 or not isinstance(b, int) or b > 0:
                    act.wait_ge(pt_mm, NH * b + k - 2)
                act.activation(PR[0:T, k % 3, 0:S], SCO[0:T, k % 3, 0:S], ACT.Exp, bias=MN[0:T, k:k + 1],
                               scale=-1.0, accum_out=SM[0:T, k:k + 1]).then_inc(prob, 1)

            def probs_out(b, k):
                act.wait_ge(pt_mm, NH * b + k + 1)
                h = k // HALF
                if k % HALF == 0:
                    wait_from(act, pv, NHALF * b + h - 1)
                act.activation(PT[0:SP, h % 2, k % HALF, :], TP[0:SP, k % 2, 0:SC * T], ACT.Copy).then_inc(pt_act, 1)

            def unit_sums(b, u, width):
                act.wait_ge(sums_t, 3 * b + u + 1)
                src = OA[:, 2 * T:4 * T] if u < 2 else PJ[:, 0, 0:C * T]
                act.activation(RI[:, 0:width], src, ACT.Copy).then_inc(inv, 1)

            def values1(b, s, bank):
                act.wait_ge(v1_mm, 3 * b + s + 1)
                act.activation(V1[0:SP, s, :], bank, ACT.Copy).then_inc(v1_ev, 1)

            act.wait_ge(l_sm, 16 * 9)
            act.activation(GT[:, 1:2], GT[:, 0:1], ACT.Tanh).then_inc(gate_t, 1)
            act.wait_ge(l_q1, 16)
            act.activation(BQ0[:, :], BQ0[:, :], ACT.Copy, scale=SCALE0).then_inc(w_q0b, 1)
            act.activation(WQ0[:, :, :], WQ0[:, :, :], ACT.Copy, scale=SCALE0).then_inc(w_q0, 1)
            act.wait_ge(w_q0b, 1)
            keys0_high(0)
            queries0_high(0)

            def batch(b, first, more):
                for k in range(35):
                    if k == 0 and not first:
                        exps(b - 1, NH - 1)
                    if 1 <= k <= 32:
                        exps(b, k - 1)
                    if k in (1, 2) and not first:
                        probs_out(b - 1, NH - 3 + k)
                    if k >= 3 and (k - 3) % 4 != 1:
                        probs_out(b, k - 3)
                    if k in (1, 3, 5, 7):
                        c = k // 2
                        act.wait_ge(at_ev, 4 * b + c + 1)
                        act.wait_ge(v0_mm, b + 1)
                        act.activation(TH[:, c, 0:SC * SP], AT[:, c, 0:SC * SP], ACT.Copy).then_inc(at_h, 1)
                    if k == 6 and not first:
                        unit_sums(b - 1, 2, C * T)
                    if k == 22:
                        unit_sums(b, 0, 2 * T)
                    if k - 1 in K1_DONE:
                        m = K1_DONE.index(k - 1)
                        act.wait_ge(k1_mm, 4 * b + m + 1)
                        if m >= 2:
                            act.wait_ge(k1st[0], 32 * b + 32)
                        elif not first:
                            act.wait_ge(k1st[1], 32 * b)
                        act.activation(K1HL[:, 0, m % 2, :], PJ[:, m % 2, 0:SW], ACT.Copy).then_inc(k1_h, 1)
                unit_sums(b, 1, 2 * T)
                values1(b, 0, PJ[0:SP, 1, :])
                values1(b, 1, SCO[0:SP, 0, :])
                act.wait_ge(yt_mm, b + 1)
                act.activation(YT[:, :, :].rearrange("p c t -> p (c t)"), PJ[:, 0, 0:C * T], ACT.Copy)\
                    .then_inc(yt_ev, 1)
                act.wait_ge(q1_mm, b + 1)
                act.wait_ge(qst, 32 * b + 32)
                act.activation(QHL[:, 0, :, :].rearrange("p m t -> p (m t)"), PJ[:, 1, 0:C * T], ACT.Copy)\
                    .then_inc(q1_h, 1)
                for j in (0, 2):
                    act.wait_ge(rep_mm, 4 * b + j + 1)
                    act.activation(Q1S[:, j, :, :].rearrange("p m t -> p (m t)"), REP_BANK[j], ACT.Copy)\
                        .then_inc(rep_act, 1)
                values1(b, 2, SCO[0:SP, 1, :])
                for k in range(33, NH):
                    exps(b, k - 1)
                    if k >= 35 and (k - 3) % 4 != 1:
                        probs_out(b, k - 3)
                    if more and k == 36:
                        queries0_high(b + 1)
                    if more and k == 40:
                        keys0_high(b + 1)

            batch(0, True, True)
            with act.Fori(1, NB - 1) as b:
                batch(b, False, True)
            batch(NB - 1, False, False)
            exps(NB - 1, NH - 1)
            for k in (NH - 2, NH - 1):
                probs_out(NB - 1, k)
            unit_sums(NB - 1, 2, C * T)

        @block.gpsimd
        def _(pool):
            def split_ctx_low(q):
                pool.wait_ge(ct_h, q + 1)
                pool.tensor_tensor(TL[:, 2:4, :], AT[:, 2:4, :], TH[:, 2:4, :].bitcast(F32), ALU.subtract)\
                    .then_inc(ct_l, 1)

            def ctx_rstd(q):
                pool.wait_ge(c_mv, 3 * q + 3)
                pool.sem_inc(met_pool, 1)
                pool.tensor_scalar(CVE[0:SP, :], CMV[0:SP, :, 1], EPS1, None, ALU.add).then_inc(c_ve, 1)
                pool.wait_ge(c_ve, q + 1)
                pool.tensor_tensor(CRS[0:SP, :], CVE[0:SP, :], mhalf[0:SP, :], ALU.pow).then_inc(c_rs, 1)

            split_ctx_low(0)
            ctx_rstd(0)

            def batch(b, more):
                for c in range(C):
                    pool.wait_ge(at_h, 4 * b + c + 1)
                    pool.tensor_tensor(TL[:, c, 0:SC * SP], AT[:, c, 0:SC * SP], TH[:, c, 0:SC * SP].bitcast(F32),
                                       ALU.subtract).then_inc(at_l, 1)
                pool.wait_ge(l_mk1, 16 * b + 16)
                wait_from(pool, shifted, NH * b)
                pool.sem_inc(met_pool, 1)
                pool.tensor_scalar(MK1[0:T, :], MU[0:T, :], -1.0, BIG, ALU.add, ALU.mult).then_inc(mk1_a, 1)
                pool.wait_ge(mk1_a, b + 1)
                pool.sem_inc(met_pool, 1)
                pool.tensor_scalar(MK1[0:T, :], MK1[0:T, :], BIG, None, ALU.mult).then_inc(mk1_b, 1)
                pool.wait_ge(l_xn, 16 * b + 16)
                pool.tensor_tensor(XN[0:T, :], XN[0:T, :], BO0[0:T, :], ALU.add).then_inc(xb, 1)
                if more:
                    ctx_rstd(b + 1)
                pool.wait_ge(y_mv, b + 1)
                pool.sem_inc(met_pool, 1)
                pool.tensor_scalar(YVE[0:T, :], YMV[0:T, 1:2], EPS0, None, ALU.add).then_inc(y_ve, 1)
                pool.wait_ge(y_ve, b + 1)
                pool.tensor_tensor(YRS[0:T, :], YVE[0:T, :], mhalf[0:T, 0:1], ALU.pow).then_inc(y_rs, 1)
                if more:
                    split_ctx_low(b + 1)

            batch(0, True)
            with pool.Fori(1, NB - 1) as b:
                batch(b, True)
            batch(NB - 1, False)


def kernel(**inputs):
    import numpy as np
    import concourse.bacc as bacc
    from concourse.bass_utils import run_bass_kernel_spmd

    a = {k: np.asarray(v) for k, v in inputs.items()}
    D, C, KVH, HD, GR = 512, 4, 8, 16, 4

    def chunked(w):
        return w.reshape(C, 128, -1).transpose(1, 0, 2)

    wq0 = a["L0_xattn_Wq"].reshape(D, 2, 4, GR, HD).transpose(0, 3, 1, 4, 2).reshape(D, D)
    wk0 = a["L0_xattn_Wk"].reshape(D, 2, 4, HD).transpose(0, 1, 3, 2).reshape(D, KVH * HD)
    wo0 = a["L0_xattn_Wo"].reshape(2, 4, 2, 2, HD, D).transpose(1, 2, 4, 0, 3, 5).reshape(128, C, D)
    bq0 = a["L0_xattn_bq"].reshape(2, 4, GR, HD).transpose(0, 3, 1, 2).reshape(128, GR)
    bk0 = a["L0_xattn_bk"].reshape(2, 4, HD).transpose(0, 2, 1).reshape(128, 1)
    repeat = np.zeros((4, 32, 2, 4, 32), np.float32)
    for r in range(4):
        repeat[:, range(32), r // 2, r, range(32)] = 1.0
    repeat = repeat.reshape(128, 2, 128)
    x, c = a["x"], a["ctx_2048"]
    arrays = {
        "x_rows": x,
        "x_cols": x.transpose(0, 2, 1).reshape(x.shape[0], C, 128, x.shape[1]).transpose(0, 2, 1, 3),
        "ctx_rows": c,
        "ctx_cols": c.transpose(0, 2, 1).reshape(c.shape[0], C, 128, c.shape[1]).transpose(0, 2, 1, 3),
        "mask0": a["mask_Bx1xSxS2_ff0"][:, 0],
        "mask1": a["mask_BxS2_bf1"],
        "wq0": chunked(wq0), "wk0": chunked(wk0), "wv0": chunked(a["L0_xattn_Wv"]), "wo0": wo0,
        "bq0": bq0, "bk0": bk0, "bv0": a["L0_xattn_bv"], "bo0": a["L0_xattn_bo"],
        "gamma0": a["L0_xattn_gamma"], "beta0": a["L0_xattn_beta"],
        "wq1": chunked(a["L1_xattn_Wq"].T), "wk1": chunked(a["L1_xattn_Wk"].T),
        "wv1": chunked(a["L1_xattn_Wv"].T), "wo1": chunked(a["L1_xattn_Wo"].T),
        "gamma1": a["L1_xattn_ln_gamma"].reshape(C, 128).T, "beta1": a["L1_xattn_ln_beta"].reshape(C, 128).T,
        "gate": a["L1_xattn_gate"],
        "identity": np.eye(128, dtype=np.float32),
        "repeat": repeat,
    }
    arrays = {k: np.ascontiguousarray(v) for k, v in arrays.items()}
    nc = bacc.Bacc("TRN2", target_bir_lowering=False, num_devices=1)
    args = [nc.dram_tensor(k, v.shape, mybir.dt.from_np(v.dtype), kind="ExternalInput").ap() for k, v in arrays.items()]
    out = nc.dram_tensor("out", x.shape, mybir.dt.float32, kind="ExternalOutput").ap()
    two_layer_cross_attention(nc, *args, out)
    r = run_bass_kernel_spmd(nc, [arrays], core_ids=[0])
    return r.results[0]["out"]
```

```python
from contextlib import ExitStack

import concourse.bass as bass
from concourse import mybir

F32 = mybir.dt.float32
F32R = mybir.dt.float32r
U8 = mybir.dt.uint8
ALU = mybir.AluOpType
ACT = mybir.ActivationFunctionType

P = 128
BIG = 3.0e38


def wait_from(engine, semaphore, count):
    if not isinstance(count, int) or count > 0:
        engine.wait_ge(semaphore, count)


def two_layer_cross_attention(nc, x_rows, x_cols, ctx_rows, ctx_cols, mask0, mask1,
                              wq0, wk0, wv0, wo0, wq1, wk1, wv1, wo1, columns, rows, identity, repeat, out):
    NB, T, D = x_rows.shape
    S = ctx_rows.shape[1]
    C = D // P
    KVH, HD0 = 8, 16
    GR = D // (KVH * HD0)
    HD1 = 32
    SC = 3
    SP = -(-S // SC)
    SE = S + (S & 1)
    SW = 364
    NH = 48
    HALF = 8
    NHALF = NH // HALF
    NJ = 4
    ACT_OUTS, DVE_OUTS = 36, 12
    EPS0, EPS1 = 1e-6, 1e-5
    SCALE0, SCALE1 = HD0 ** -0.5, HD1 ** -0.5
    assert SC * SP <= SW and D == C * P and KVH * HD0 == P and SE <= 512

    with ExitStack() as ctx:
        def sb(name, shape, dt=F32):
            return ctx.enter_context(nc.sbuf_tensor(name, shape, dt))

        def sem(name):
            return ctx.enter_context(nc.semaphore(name))

        WQ0 = sb("WQ0", [P, C, D])
        WO0 = sb("WO0", [P, C, D])
        WQ1 = sb("WQ1", [P, C, D])
        WO1 = sb("WO1", [P, C, D])
        WK0h, WK0l = sb("WK0h", [P, C, P], F32R), sb("WK0l", [P, C, P], F32R)
        WV0h, WV0l = sb("WV0h", [P, C, P], F32R), sb("WV0l", [P, C, P], F32R)
        WK1h, WK1l = sb("WK1h", [P, C, D], F32R), sb("WK1l", [P, C, D], F32R)
        WV1h, WV1l = sb("WV1h", [P, C, D], F32R), sb("WV1l", [P, C, D], F32R)
        COLS = sb("COLS", [P, GR + 1 + 2 * C])
        BQ0, BK0, G1, B1 = (COLS[:, 0:GR], COLS[:, GR:GR + 1], COLS[:, GR + 1:GR + 1 + C],
                            COLS[:, GR + 1 + C:GR + 1 + 2 * C])
        ROWS = sb("ROWS", [P, P + 3 * D + 1])
        BV0, BO0, G0, B0 = (ROWS[:, 0:P], ROWS[:, P:P + D], ROWS[:, P + D:P + 2 * D], ROWS[:, P + 2 * D:P + 3 * D])
        GT = ROWS[:, P + 3 * D:P + 3 * D + 1]
        ident = sb("ident", [P, P])
        mhalf = sb("mhalf", [P, SC])

        AT = sb("AT", [P, C, SW])
        TH, TL = sb("TH", [P, C, SW], F32R), sb("TL", [P, C, SW], F32R)
        NAT = sb("NAT", [P, SC, D])
        CST, CMV, CVE, CRS = sb("CST", [P, SC, 6]), sb("CMV", [P, SC, 2]), sb("CVE", [P, SC]), sb("CRS", [P, SC])
        K1HL = sb("K1HL", [P, 3, 2, SW], F32R)
        K1S = sb("K1S", [P, NJ, C, SW], F32R)
        V1 = sb("V1", [P, SC, D])
        KHL = sb("KHL", [P, 2, SW], F32R)
        V0T = sb("V0T", [P, SC * SP])
        K0S = sb("K0S", [P, 4, SW], F32R)
        V0P = sb("V0P", [P, SC, KVH, 3 * HD0])
        XT = sb("XT", [P, C, T])
        QHL = sb("QHL", [P, 2, GR, T], F32R)
        Q1S = sb("Q1S", [P, NJ, C, T], F32R)
        RP = sb("RP", [P, 2, P], F32R)
        Q0S = sb("Q0S", [P, 4, GR, T], F32R)
        MK0, MU, MK1 = sb("MK0", [P, S]), sb("MU", [P, S], U8), sb("MK1", [P, S])
        PR = sb("PR", [P, 3, SW])
        MN, SM = sb("MN", [P, NH]), sb("SM", [P, NH])
        PT = sb("PT", [P, 2, HALF, SC * T])
        V1_flat = V1[:, :, :].rearrange("p a b -> p (a b)")
        PT_flat = PT[:, :, :, :].rearrange("p a b c -> p (a b c)")
        WV1_AT = HALF * SC * T
        RSM = sb("RSM", [P, 16])
        SX = sb("SX", [P, C, P])
        RI = SX[:, :, :].rearrange("p a b -> p (a b)")
        OT = sb("OT", [P, C, T])
        R0, Y = sb("R0", [P, D]), sb("Y", [P, D])
        YST, YMV, YVE, YRS = sb("YST", [P, 6]), sb("YMV", [P, 2]), sb("YVE", [P, 1]), sb("YRS", [P, 1])
        YT = OT

        k_scr = nc.dram_tensor("k_scr", (2, 2, P // 2, SW), F32, kind="Internal").ap()
        k1_scr = nc.dram_tensor("k1_scr", (2, 2, P, 2, SW), F32, kind="Internal").ap()
        q_scr = nc.dram_tensor("q_scr", (2, P, GR * T), F32, kind="Internal").ap()

        SCO = ctx.enter_context(nc.psum_tensor("SCO", [P, 3, 512], F32))
        TP = ctx.enter_context(nc.psum_tensor("TP", [P, 2, 512], F32))
        OA = ctx.enter_context(nc.psum_tensor("OA", [P, 512], F32))
        PJ = ctx.enter_context(nc.psum_tensor("PJ", [P, 2, 512], F32))

        l_k0, l_v0, l_q1, l_k1, l_v1, l_o = (sem("l_k0"), sem("l_v0"), sem("l_q1"), sem("l_k1"), sem("l_v1"),
                                             sem("l_o"))
        l_sm, l_row, l_rp = sem("l_sm"), sem("l_row"), sem("l_rp")
        l_ct, l_nat, l_xt, l_xn = sem("l_ct"), sem("l_nat"), sem("l_xt"), sem("l_xn")
        l_mk0, l_mk1 = sem("l_mk0"), sem("l_mk1")
        kst, kld, qld = ([sem(f"{n}{par}") for par in range(2)] for n in ("kst", "kld", "qld"))
        k1st, k1ld = ([sem(f"{n}{half}") for half in range(2)] for n in ("k1st", "k1ld"))
        qst, ost, l_id = sem("qst"), sem("ost"), sem("l_id")
        rep_id, rep_mm, rep_act, rep_dve = sem("rep_id"), sem("rep_mm"), sem("rep_act"), sem("rep_dve")
        k0w_h, v0w_h, k1w_h, v1w_h = sem("k0w_h"), sem("v0w_h"), sem("k1w_h"), sem("v1w_h")
        k0w_l, v0w_l, k1w_l, v1w_l, w_q0 = sem("k0w_l"), sem("v0w_l"), sem("k1w_l"), sem("v1w_l"), sem("w_q0")
        gate_t, w_q0b, pad_zero, nat_zero = sem("gate_t"), sem("w_q0b"), sem("pad_zero"), sem("nat_zero")
        pool_zero = sem("pool_zero")
        ct_h, ct_h2, ct_l, ct_l2, th_free = sem("ct_h"), sem("ct_h2"), sem("ct_l"), sem("ct_l2"), sem("th_free")
        k0_mm, k0_h, k0_l = sem("k0_mm"), sem("k0_h"), sem("k0_l")
        q0_mm, q0_h, q0_l = sem("q0_mm"), sem("q0_h"), sem("q0_l")
        v0_mm, v0_t, v0_tr, v0_ev = sem("v0_mm"), sem("v0_t"), sem("v0_tr"), sem("v0_ev")
        c_st, c_mv, c_ve, c_rs, c_nrm = sem("c_st"), sem("c_mv"), sem("c_ve"), sem("c_rs"), sem("c_nrm")
        at_mm, at_ev, at_h, at_l = sem("at_mm"), sem("at_ev"), sem("at_h"), sem("at_l")
        k1_mm, k1_h, k1_l = sem("k1_mm"), sem("k1_h"), sem("k1_l")
        v1_mm, v1_ev = sem("v1_mm"), sem("v1_ev")
        mk1_a, mk1_b = sem("mk1_a"), sem("mk1_b")
        scored, shifted, prob = sem("scored"), sem("shifted"), sem("prob")
        pt_mm, pt_act, pt_dve = sem("pt_mm"), sem("pt_act"), sem("pt_dve")
        rcp, sums_x = sem("rcp"), sem("sums_x")
        pv, sums_t, inv, attn = sem("pv"), sem("sums_t"), sem("inv"), sem("attn")
        xb, out0_mm, res, y_st, y_mv, y_ve, y_rs = (sem("xb"), sem("out0_mm"), sem("res"), sem("y_st"),
                                                    sem("y_mv"), sem("y_ve"), sem("y_rs"))
        y_n, y_ok, yt_mm, yt_ev = sem("y_n"), sem("y_ok"), sem("yt_mm"), sem("yt_ev")
        q1_mm, q1_h, q1_l, out1_mm, fin = sem("q1_mm"), sem("q1_h"), sem("q1_l"), sem("out1_mm"), sem("fin")

        met_dve, met_pool, met_sp = sem("met_dve"), sem("met_pool"), sem("met_sp")

        def spans(counts):
            ends = {}
            at = 0
            for k in sorted(counts):
                ends[k] = (at, at + counts[k])
                at += counts[k]
            return ends

        K1_STEPS = spans({7: 2, 8: 1, 9: 1, 10: 1, 13: 1, 14: 1, 15: 1, 16: 2, 17: 2, 18: 3, 19: 2, 20: 2, 21: 2,
                          22: 3, 23: 3, 24: 3, 25: 3, 26: 3, 27: 2, 28: 2, 29: 2, 30: 3, 31: 3})
        Q0_STEPS = spans({32: 5, 33: 4, 34: 3, 35: 2, 36: 2})
        K0_STEPS = spans({34: 1, 35: 2, 36: 3, 37: 3, 38: 3})
        V0_STEPS = spans({40: 3, 41: 3, 42: 3, 43: 3})
        K1_DONE = [max(k for k, (i, _) in K1_STEPS.items() if i < 12 * (m + 1)) for m in range(C)]
        REP_BANK = (SCO[:, 2, 0:C * T], TP[:, 0, 0:C * T], TP[:, 1, 0:C * T], SCO[:, 0, 0:C * T])

        def copied_out(b, k):
            if k % 4 == 1:
                return pt_dve, DVE_OUTS * b + (k + 3) // 4
            return pt_act, ACT_OUTS * b + k + 1 - (k + 3) // 4

        def flat(w):
            return w[:, :, :].rearrange("p c n -> p (c n)")

        block = ctx.enter_context(nc.Block())

        @block.sync
        def _(sp):
            def load_ctx_cols(q):
                sp.dma_start(AT[:, :, 0:S], ctx_cols[q]).then_inc(l_ct, 16)

            def load_ctx_rows(q):
                full = (SC - 1) * SP
                sp.dma_start(NAT[0:SP, 0:SC - 1, :],
                             ctx_rows[q, 0:full, :].rearrange("(c p) d -> p c d", p=SP)).then_inc(l_nat, 16)
                sp.dma_start(NAT[0:S - full, SC - 1, :], ctx_rows[q, full:S, :]).then_inc(l_nat, 16)

            def spread_heads0(q):
                sp.wait_ge(q0_h, 4 * q + 4)
                sp.wait_ge(q0_l, 4 * q + 4)
                sp.dma_start(q_scr.rearrange("h p t -> p h t"),
                             QHL[:, :, :, :].bitcast(F32).rearrange("p h g t -> p h (g t)")).then_inc(qst, 16)
                sp.wait_ge(k0_h, q + 1)
                sp.wait_ge(k0_l, q + 1)
                for par in range(2):
                    sp.dma_start(k_scr[par].rearrange("h p s -> p h s"), KHL[64 * par:64 * par + 64, :, :].bitcast(F32))\
                        .then_inc(kst[par], 16)
                sp.wait_ge(qst, 16 * q + 16)
                for par in range(2):
                    for hl in range(2):
                        at = 64 * par + 32 * hl
                        src = q_scr[hl, 64 * par:64 * par + 64, :].rearrange("(d i) t -> d (i t)", i=4)
                        dst = Q0S[at:at + 32, :, :, :].bitcast(F32).rearrange("d i g t -> d (i g t)")
                        sp.dma_start(dst, src.unsqueeze(0).to_broadcast([2, 16, 4 * GR * T])).then_inc(qld[par], 16)
                    sp.wait_ge(kst[par], 16 * q + 16)
                    src = k_scr[par].rearrange("a (d i) s -> (a d) (i s)", i=4)
                    dst = K0S[64 * par:64 * par + 64, :, :].bitcast(F32).rearrange("d i s -> d (i s)")
                    sp.dma_start(dst, src.unsqueeze(0).to_broadcast([2, 32, 4 * SW])).then_inc(kld[par], 16)

            def store_keys1(b, m):
                sp.wait_ge(k1_h, 4 * b + m + 1)
                sp.wait_ge(k1_l, 4 * b + m + 1)
                dst = k1_scr[:, m // 2, :, m % 2, :].rearrange("h p s -> p h s")
                sp.dma_start(dst, K1HL[:, m % 3, :, :].bitcast(F32)).then_inc(k1st[m // 2], 16)

            def load_keys1(b, half):
                sp.wait_ge(k1st[half], 32 * b + 32)
                for term in range(4):
                    src = k1_scr[term % 2, half].rearrange("(j d) m f -> d j (m f)", d=HD1)
                    dst = K1S[32 * term:32 * term + 32, :, 2 * half:2 * half + 2, :].bitcast(F32)
                    sp.dma_start(dst.rearrange("d j m s -> d j (m s)"), src).then_inc(k1ld[half], 16)

            sp.dma_start(V1_flat[:, 0:C * P], wk0.rearrange("p c n -> p (c n)")).then_inc(l_k0, 16)
            load_ctx_cols(0)
            sp.dma_start(COLS[:, :], columns).then_inc(l_sm, 16)
            sp.dma_start(WQ0[:, :, :], wq0).then_inc(l_q1, 16)
            sp.dma_start(XT[:, :, :], x_cols[0]).then_inc(l_xt, 16)
            sp.dma_start(V1_flat[:, C * P:2 * C * P], wv0.rearrange("p c n -> p (c n)")).then_inc(l_v0, 16)
            sp.wait_ge(nat_zero, 1)
            load_ctx_rows(0)
            sp.dma_start(PT_flat[:, 0:C * D], wk1.rearrange("p c n -> p (c n)")).then_inc(l_k1, 16)
            sp.dma_start(ROWS[:, :], rows.partition_broadcast(P)).then_inc(l_row, 16)
            sp.dma_start(ident[:, :], identity).then_inc(l_id, 16)
            sp.dma_start(MK0[0:T, :], mask0[0]).then_inc(l_mk0, 16)
            sp.dma_start(PT_flat[:, WV1_AT:WV1_AT + C * D], wv1.rearrange("p c n -> p (c n)")).then_inc(l_v1, 16)
            sp.dma_start(SX[:, 0:2, :], repeat).then_inc(l_rp, 16)
            spread_heads0(0)
            sp.dma_start(MU[0:T, :], mask1[0].partition_broadcast(T)).then_inc(l_mk1, 16)
            sp.dma_start(R0[0:T, :], x_rows[0]).then_inc(l_xn, 16)
            sp.dma_start(WO0[:, :, :], wo0).then_inc(l_o, 16)
            sp.dma_start(WQ1[:, :, :], wq1).then_inc(l_o, 16)
            sp.dma_start(WO1[:, :, :], wo1).then_inc(l_o, 16)

            def batch(b, first):
                sp.wait_ge(q0_mm, b + 1)
                sp.dma_start(XT[:, :, :], x_cols[b + 1]).then_inc(l_xt, 16)
                sp.wait_ge(at_mm, 4 * b + 4)
                load_ctx_rows(b + 1)
                sp.wait_ge(at_h, 4 * b + 4)
                sp.wait_ge(at_l, 4 * b + 4)
                load_ctx_cols(b + 1)
                sp.wait_ge(mk1_a, b + 1)
                sp.sem_inc(met_sp, 1)
                sp.dma_start(MU[0:T, :], mask1[b + 1].partition_broadcast(T)).then_inc(l_mk1, 16)
                store_keys1(b, 0)
                if not first:
                    sp.wait_ge(fin, b)
                    sp.dma_start(out[b - 1], R0[0:T, :]).then_inc(ost, 16)
                store_keys1(b, 1)
                load_keys1(b, 0)
                if not first:
                    sp.wait_ge(ost, 16 * b)
                    sp.dma_start(R0[0:T, :], x_rows[b]).then_inc(l_xn, 16)
                store_keys1(b, 2)
                store_keys1(b, 3)
                load_keys1(b, 1)
                sp.wait_ge(shifted, NH * b + 32)
                sp.dma_start(MK0[0:T, :], mask0[b + 1]).then_inc(l_mk0, 16)
                spread_heads0(b + 1)

            batch(0, True)
            with sp.Fori(1, NB - 1) as b:
                batch(b, False)
            store_keys1(NB - 1, 0)
            sp.wait_ge(fin, NB - 1)
            sp.dma_start(out[NB - 2], R0[0:T, :]).then_inc(ost, 16)
            store_keys1(NB - 1, 1)
            load_keys1(NB - 1, 0)
            sp.wait_ge(ost, 16 * (NB - 1))
            sp.dma_start(R0[0:T, :], x_rows[NB - 1]).then_inc(l_xn, 16)
            store_keys1(NB - 1, 2)
            store_keys1(NB - 1, 3)
            load_keys1(NB - 1, 1)
            sp.wait_ge(fin, NB)
            sp.dma_start(out[NB - 1], R0[0:T, :]).then_inc(ost, 16)
            sp.wait_ge(ost, 16 * NB)

        @block.tensor
        def _(pe):
            def mm3(dst, wh, wl, xh, xl, start, stop):
                pe.matmul(dst, wh, xh, start=start, stop=False)
                pe.matmul(dst, wl, xh, start=False, stop=False)
                return pe.matmul(dst, wh, xl, start=False, stop=stop)

            def mm3_step(term, dst, wh, wl, xh, xl, start, stop):
                w, x = ((wh, xh), (wl, xh), (wh, xl))[term]
                return pe.matmul(dst, w, x, start=start and term == 0, stop=stop and term == 2)

            def keys0(steps=range(3 * C)):
                for i in steps:
                    c, term = divmod(i, 3)
                    last = mm3_step(term, PJ[:, 1, 0:SW], WK0h[:, c, :], WK0l[:, c, :], TH[:, c, :], TL[:, c, :],
                                    c == 0, c == C - 1)
                    if i == 3 * C - 1:
                        last.then_inc(k0_mm, 1)

            def queries0(steps=range(GR * C)):
                for i in steps:
                    g, c = divmod(i, C)
                    last = pe.matmul(PJ[:, 0, g * T:(g + 1) * T], WQ0[:, c, g * P:(g + 1) * P],
                                     XT[:, c, :], start=c == 0, stop=c == C - 1)
                    if i == GR * C - 1:
                        last.then_inc(q0_mm, 1)

            def values0(bank=PJ[:, 0, :], steps=range(3 * C)):
                for i in steps:
                    c, term = divmod(i, 3)
                    last = mm3_step(term, bank[:, 0:SW], WV0h[:, c, :], WV0l[:, c, :], TH[:, c, :], TL[:, c, :],
                                    c == 0, c == C - 1)
                    if i == 3 * C - 1:
                        last.then_inc(v0_mm, 1)

            def values0_transposed(q, bank=PJ[:, 0, :]):
                pe.wait_ge(v0_t, q + 1)
                for c in range(SC):
                    last = pe.transpose(bank[0:SP, c * P:(c + 1) * P], V0T[:, c * SP:(c + 1) * SP], ident[:, :])
                last.then_inc(v0_tr, 1)

            def score(b, k):
                dst = SCO[0:T, k % 3, 0:SE]
                if k < 32:
                    G, gh, gl, j = k // 16, k // 8 % 2, k // 4 % 2, k % 4
                    pe.matmul(dst, Q0S[64 * G:64 * G + 64, j, 2 * gh + gl, :], K0S[64 * G:64 * G + 64, j, 0:SE],
                              start=True, stop=True).then_inc(scored, 1)
                else:
                    m, j = (k - 32) // 4, k % 4
                    pe.matmul(dst, Q1S[:, j, m, :], K1S[:, j, m, 0:SE], start=True, stop=True).then_inc(scored, 1)

            def transpose_probs(b, k):
                pe.wait_ge(prob, NH * b + k + 1)
                for c in range(SC):
                    last = pe.transpose(TP[0:SP, k % 2, c * T:(c + 1) * T], PR[0:T, k % 3, c * SP:(c + 1) * SP],
                                        ident[0:T, 0:T])
                last.then_inc(pt_mm, 1)

            def free_tp(b, k):
                if k >= 2:
                    pe.wait_ge(*copied_out(b, k - 2))
                elif not isinstance(b, int) or b > 0:
                    pe.wait_ge(*copied_out(b - 1, k - 2 + NH))

            def out_half(b, h, parts):
                for part in parts:
                    ml, c = divmod(part, SC)
                    if part == 0:
                        pe.wait_ge(pt_act, ACT_OUTS * b + 6 * h + 6)
                        pe.wait_ge(pt_dve, DVE_OUTS * b + 2 * h + 2)
                        if h % 2 == 0:
                            wait_from(pe, attn, 3 * b + h // 2)
                    for j in range(NJ):
                        if h < 4:
                            G, gh = h // 2, h % 2
                            lhs = V0P[0:SP, c, 4 * G + j, (HD0, 0)[gh]:(HD0, 0)[gh] + 32]
                            rhs = PT[0:SP, h % 2, :, c * T:(c + 1) * T].rearrange("p (a j) t -> p a j t", j=NJ)[:, :, j, :]
                            last = pe.matmul(OA[32 * j:32 * j + 32, 0:2 * T], lhs, rhs,
                                             start=gh == 0 and c == 0, stop=gh == 1 and c == SC - 1)
                        else:
                            m = 2 * (h - 4) + ml
                            head = 4 * m + j
                            last = pe.matmul(OA[32 * j:32 * j + 32, m * T:(m + 1) * T],
                                             V1[0:SP, c, head * HD1:(head + 1) * HD1],
                                             PT[0:SP, h % 2, 4 * ml + j, c * T:(c + 1) * T],
                                             start=c == 0, stop=c == SC - 1)
                    if part == (2 if h < 4 else 5):
                        last.then_inc(pv, 1)

            def sums_transposed(b, u):
                dst = OA[:, 2 * T:4 * T] if u < 2 else PJ[:, 0, :]
                pe.wait_ge(sums_x, 3 * b + u + 1)
                for m in range(2 if u < 2 else C):
                    last = pe.transpose(dst[:, m * T:(m + 1) * T], SX[0:T, m, :], ident[0:T, 0:T])
                last.then_inc(sums_t, 1)

            def out0(b):
                for c in range(C):
                    last = pe.matmul(PJ[0:T, 1, :], OT[:, c, :], WO0[:, c, :], start=c == 0, stop=c == C - 1)
                last.then_inc(out0_mm, 1)

            def out1(b, steps):
                for i in steps:
                    half, c = divmod(i, C)
                    cols = slice(half * (D // 2), (half + 1) * (D // 2))
                    last = pe.matmul(PJ[0:T, 1, cols], OT[:, c, :], WO1[:, c, cols], start=c == 0, stop=c == C - 1)
                    if i == 2 * C - 1:
                        last.then_inc(out1_mm, 1)

            def ctx_transposed(b, c):
                for s in range(SC):
                    last = pe.transpose(PJ[:, c % 2, s * SP:(s + 1) * SP], NAT[0:SP, s, c * P:(c + 1) * P],
                                        ident[0:SP, 0:SP])
                last.then_inc(at_mm, 1)

            def keys1(b, i):
                m, c, term = i // (3 * C), i // 3 % C, i % 3
                cols = slice(m * P, (m + 1) * P)
                last = mm3_step(term, PJ[:, m % 2, 0:SW], WK1h[:, c, cols], WK1l[:, c, cols], TH[:, c, :],
                                TL[:, c, :], c == 0, c == C - 1)
                if i % (3 * C) == 3 * C - 1:
                    last.then_inc(k1_mm, 1)

            V1_BANK = (PJ[0:SP, 0, :], SCO[0:SP, 0, :], SCO[0:SP, 1, :])

            def values1(b, steps):
                for i in steps:
                    s, c = divmod(i, C)
                    rows = slice(s * SP, (s + 1) * SP)
                    last = mm3(V1_BANK[s], TH[:, c, rows], TL[:, c, rows], WV1h[:, c, :], WV1l[:, c, :],
                               c == 0, c == C - 1)
                    if c == C - 1:
                        last.then_inc(v1_mm, 1)
                    elif s == SC - 1:
                        last.then_inc(th_free, 1)

            pe.wait_ge(pad_zero, 1)
            pe.wait_ge(k0w_l, 1)
            pe.wait_ge(ct_h, 2)
            pe.wait_ge(ct_l2, 2)
            keys0(range(6))
            pe.wait_ge(ct_l, 1)
            keys0(range(6, 12))
            pe.wait_ge(w_q0, 1)
            pe.wait_ge(l_xt, 16)
            queries0()
            pe.wait_ge(v0w_l, 1)
            values0(SCO[:, 2, :])
            pe.wait_ge(l_id, 16)
            values0_transposed(0, SCO[:, 2, :])

            def batch(b, first, more):
                for k in range(34):
                    if k < 32:
                        if k % 16 == 0:
                            pe.wait_ge(kld[k // 16], 16 * b + 16)
                            pe.wait_ge(qld[k // 16], 32 * b + 32)
                        if k >= 3 or not first:
                            pe.wait_ge(prob, NH * b + k - 2)
                        score(b, k)
                    if k in (0, 2, 4, 6):
                        c = k // 2
                        if c == 0:
                            pe.wait_ge(c_nrm, 3 * b + 3)
                            pe.wait_ge(v0_ev, b + 1)
                        elif c == 1:
                            pe.wait_ge(k0_l, b + 1)
                        else:
                            pe.wait_ge(at_ev, 4 * b + c - 1)
                        ctx_transposed(b, c)
                    if k < 2 and not first:
                        free_tp(b - 1, NH - 2 + k)
                        transpose_probs(b - 1, NH - 2 + k)
                        out_half(b - 1, 4, range(k + 4, k + 5))
                    if k >= 2:
                        free_tp(b, k - 2)
                        transpose_probs(b, k - 2)
                    if k in (3, 4, 5) and not first:
                        out_half(b - 1, 5, range(2 * (k - 3), 2 * (k - 3) + 2))
                        if k == 5:
                            pe.wait_ge(at_ev, 4 * b + 3)
                            sums_transposed(b - 1, 2)
                    if 8 <= k < 16 and not first:
                        if k == 8:
                            pe.wait_ge(attn, 3 * b)
                            pe.wait_ge(at_ev, 4 * b + 4)
                        out1(b - 1, range(k - 8, k - 7))
                    if k == 7 and first:
                        pe.wait_ge(k1w_l, 1)
                    for i in range(*K1_STEPS.get(k, (0, 0))):
                        if i < 3 * C and i % 3 == 0:
                            pe.wait_ge(at_h, 4 * b + i // 3 + 1)
                            pe.wait_ge(at_l, 4 * b + i // 3 + 1)
                        if i == 0:
                            pe.wait_ge(at_ev, 4 * b + 3)
                            if not first:
                                pe.wait_ge(inv, 3 * b)
                        elif i == 3 * C:
                            pe.wait_ge(at_ev, 4 * b + 4)
                            if not first:
                                pe.wait_ge(fin, b)
                        elif i % (3 * C) == 0:
                            pe.wait_ge(k1_l, 4 * b + i // (3 * C) - 1)
                        keys1(b, i)
                    if k in (11, 12, 13, 19, 20, 21, 27, 28, 29):
                        out_half(b, (k - 11) // 8, range((k - 11) % 8, (k - 11) % 8 + 1))
                    if k == 21:
                        sums_transposed(b, 0)
                    if k in (32, 33):
                        if k == 32:
                            pe.wait_ge(k1_l, 4 * b + 3)
                            if first:
                                pe.wait_ge(v1w_l, 1)
                        values1(b, range(k - 32, k - 31))
                values1(b, range(2, 3))
                out_half(b, 3, range(3))
                sums_transposed(b, 1)
                values1(b, range(3, 4))
                pe.wait_ge(k1_l, 4 * b + 4)
                pe.wait_ge(attn, 3 * b + 2)
                if first:
                    pe.wait_ge(l_o, 48)
                    pe.wait_ge(rep_id, 1)
                out0(b)
                pe.wait_ge(prob, NH * b + 31)
                values1(b, range(4, 8))
                pe.wait_ge(prob, NH * b + 32)
                values1(b, range(8, 9))
                pe.wait_ge(y_ok, b + 1)
                for c in range(C):
                    last = pe.transpose(PJ[:, 1, c * T:(c + 1) * T], Y[0:T, c * P:(c + 1) * P], ident[0:T, 0:T])
                last.then_inc(yt_mm, 1)
                values1(b, range(9, 10))
                pe.wait_ge(v1_ev, 3 * b + 1)
                pe.wait_ge(yt_ev, b + 1)
                for m in range(C):
                    for c in range(C):
                        last = pe.matmul(PJ[:, 0, m * T:(m + 1) * T], WQ1[:, c, m * P:(m + 1) * P], YT[:, c, :],
                                         start=c == 0, stop=c == C - 1)
                last.then_inc(q1_mm, 1)
                values1(b, range(10, 12))
                pe.wait_ge(v1_ev, 3 * b + 2)
                pe.wait_ge(q1_h, b + 1)
                pe.wait_ge(q1_l, b + 1)
                for j in range(NJ):
                    r = slice(32 * j, 32 * j + 32)
                    for hl in range(2):
                        last = pe.matmul(REP_BANK[j], RP[r, hl, :], QHL[r, hl, :, :].rearrange("p m t -> p (m t)"),
                                         start=hl == 0, stop=hl == 1)
                    last.then_inc(rep_mm, 1)
                if more:
                    pe.wait_ge(l_xt, 16 * b + 32)
                for k in range(32, NH):
                    if more and k in Q0_STEPS:
                        queries0(range(*Q0_STEPS[k]))
                    if k == 32:
                        pe.wait_ge(rep_act, 2 * b + 2)
                        pe.wait_ge(rep_dve, 2 * b + 2)
                        pe.wait_ge(k1ld[0], 64 * b + 64)
                    if k == 34:
                        pe.wait_ge(v1_ev, 3 * b + 3)
                    if k == 40:
                        pe.wait_ge(k1ld[1], 64 * b + 64)
                    if k >= 35:
                        pe.wait_ge(prob, NH * b + k - 2)
                    score(b, k)
                    if more and k in K0_STEPS:
                        if k == 34:
                            pe.wait_ge(ct_l2, 2 * b + 4)
                        elif k == 36:
                            pe.wait_ge(ct_h2, b + 2)
                            pe.wait_ge(ct_l, b + 2)
                        keys0(range(*K0_STEPS[k]))
                    if more and k in V0_STEPS:
                        if k == 40:
                            pe.wait_ge(q0_l, 4 * b + 8)
                        values0(steps=range(*V0_STEPS[k]))
                    if more and k == 45:
                        values0_transposed(b + 1)
                    if k >= 34:
                        free_tp(b, k - 2)
                        transpose_probs(b, k - 2)
                    if k >= 44:
                        out_half(b, 4, range(k - 44, k - 43))

            batch(0, True, True)
            with pe.Fori(1, NB - 1) as b:
                batch(b, False, True)
            batch(NB - 1, False, False)
            for k in (NH - 2, NH - 1):
                free_tp(NB - 1, k)
                transpose_probs(NB - 1, k)
            out_half(NB - 1, 4, range(4, 6))
            out_half(NB - 1, 5, range(6))
            sums_transposed(NB - 1, 2)
            pe.wait_ge(attn, 3 * NB)
            out1(NB - 1, range(2 * C))

        @block.vector
        def _(dve):
            def split_ctx(q, c):
                dve.wait_ge(l_ct, 16 * q + 16)
                dve.tensor_copy(TH[:, c, :], AT[:, c, :]).then_inc(ct_h, 1)
                dve.wait_ge(ct_h, 2 * q + c + 1)
                dve.tensor_tensor(TL[:, c, :], AT[:, c, :], TH[:, c, :].bitcast(F32), ALU.subtract).then_inc(ct_l2, 1)

            def split_ctx_high(q):
                dve.tensor_copy(TH[:, 2:4, :], AT[:, 2:4, :]).then_inc(ct_h2, 1)

            def keys0_low(q):
                dve.wait_ge(k0_h, q + 1)
                dve.scalar_tensor_tensor(out=KHL[:, 1, :], in0=PJ[:, 1, 0:SW], scalar=BK0[:, 0:1],
                                         in1=KHL[:, 0, :].bitcast(F32), op0=ALU.add, op1=ALU.subtract)\
                    .then_inc(k0_l, 1)

            def queries0_low(q):
                for g in range(GR):
                    dve.wait_ge(q0_h, 4 * q + 4)
                    dve.scalar_tensor_tensor(out=QHL[:, 1, g, :], in0=PJ[:, 0, g * T:(g + 1) * T],
                                             scalar=BQ0[:, g:g + 1], in1=QHL[:, 0, g, :].bitcast(F32),
                                             op0=ALU.add, op1=ALU.subtract).then_inc(q0_l, 1)

            def values0(q, bank=PJ[:, 0, :]):
                dve.wait_ge(v0_tr, q + 1)
                dve.tensor_tensor(V0P[0:SP, :, :, HD0:2 * HD0],
                                  bank[0:SP, 0:SC * P].rearrange("p (s h d) -> p s h d", s=SC, h=KVH),
                                  BV0[0:SP, :].rearrange("p (h d) -> p h d", h=KVH).unsqueeze(1)
                                  .to_broadcast([SP, SC, KVH, HD0]), ALU.add)\
                    .then_inc(v0_ev, 1)

            def ctx_stats(q, s):
                if s == 0:
                    dve.wait_ge(l_nat, 32 * q + 32)
                dve.bn_stats(CST[0:SP, s, :], NAT[0:SP, s, :]).then_inc(c_st, 1)

            def ctx_mean(q):
                dve.wait_ge(c_st, 3 * q + 3)
                dve.sem_inc(met_dve, 1)
                for s in range(SC):
                    dve.bn_aggr(CMV[0:SP, s, :], CST[0:SP, s, :]).then_inc(c_mv, 1)

            def ctx_normalise(q, s):
                dve.wait_ge(c_rs, q + 1)
                dve.tensor_scalar(NAT[0:SP, s, :], NAT[0:SP, s, :], CMV[0:SP, s, 0:1], CRS[0:SP, s:s + 1],
                                  ALU.subtract, ALU.mult).then_inc(c_nrm, 1)

            def shift(b, k):
                dve.wait_ge(scored, NH * b + k + 1)
                dve.sem_inc(met_dve, 1)
                bank = SCO[0:T, k % 3, 0:S]
                mask, scale = (MK0, -1.0) if k < 32 else (MK1, -SCALE1)
                dve.tensor_tensor_reduce(out=bank, in0=bank, in1=mask[0:T, :], scale=scale, scalar=3.4e38,
                                         op0=ALU.add, op1=ALU.min, accum_out=MN[0:T, k:k + 1]).then_inc(shifted, 1)

            def probs_out(b, k):
                dve.wait_ge(pt_mm, NH * b + k + 1)
                h = k // HALF
                if k == 1 and isinstance(b, int) and b == 0:
                    dve.wait_ge(k1w_l, 1)
                if k == 9 and isinstance(b, int) and b == 0:
                    dve.wait_ge(v1w_l, 1)
                if k % HALF == 1:
                    wait_from(dve, pv, NHALF * b + h - 1)
                dve.tensor_copy(PT[0:SP, h % 2, k % HALF, :], TP[0:SP, k % 2, 0:SC * T]).then_inc(pt_dve, 1)

            def repeat_sums(b, u):
                dve.wait_ge(prob, NH * b + 16 * u + 16)
                wait_from(dve, sums_x, 3 * b + u)
                dve.reciprocal(RSM[0:T, :], SM[0:T, 16 * u:16 * u + 16]).then_inc(rcp, 1)
                wait_from(dve, attn, 3 * b + u)
                dve.wait_ge(rcp, 3 * b + u + 1)
                sums = RSM[0:T, :]
                if u < 2:
                    src = sums.rearrange("p (a g j) -> p g j a", a=2, g=2).unsqueeze(4).to_broadcast([T, 2, NJ, 2, HD0])
                    dve.tensor_copy(SX[0:T, 0:2, :].rearrange("p g (j a d) -> p g j a d", j=NJ, a=2), src)\
                        .then_inc(sums_x, 1)
                else:
                    src = sums.unsqueeze(2).to_broadcast([T, 16, HD1])
                    dve.tensor_copy(SX[0:T, :, :].rearrange("p m (j d) -> p (m j) d", j=NJ), src).then_inc(sums_x, 1)

            def unit_outputs(b, u):
                dve.wait_ge(pv, NHALF * b + 2 * u + 2)
                dve.wait_ge(inv, 3 * b + u + 1)
                n = 2 * T if u < 2 else C * T
                dst = OT[:, 2 * u:2 * u + 2, :] if u < 2 else OT[:, :, :]
                dve.tensor_tensor(dst.rearrange("p c t -> p (c t)"), OA[:, 0:n], RI[:, 0:n], ALU.mult)\
                    .then_inc(attn, 1)

            def result(b):
                dve.wait_ge(gate_t, 1)
                dve.wait_ge(out1_mm, b + 1)
                dve.scalar_tensor_tensor(out=R0[0:T, :], in0=PJ[0:T, 1, :], scalar=GT[0:T, 0:1], in1=Y[0:T, :],
                                         op0=ALU.mult, op1=ALU.add).then_inc(fin, 1)

            dve.memset(AT[:, :, S:SW], 0.0).then_inc(pad_zero, 1)
            dve.memset(NAT[:, SC - 1, :], 0.0).then_inc(nat_zero, 1)
            dve.wait_ge(pad_zero, 1)
            dve.wait_ge(k0w_h, 1)
            dve.tensor_tensor(flat(WK0l), V1_flat[:, 0:C * P], flat(WK0h).bitcast(F32), ALU.subtract)\
                .then_inc(k0w_l, 1)
            dve.wait_ge(l_ct, 16)
            split_ctx_high(0)
            for c in range(2):
                split_ctx(0, c)
            dve.wait_ge(v0w_h, 1)
            dve.tensor_tensor(flat(WV0l), V1_flat[:, C * P:2 * C * P], flat(WV0h).bitcast(F32), ALU.subtract)\
                .then_inc(v0w_l, 1)
            dve.wait_ge(l_sm, 16)
            dve.wait_ge(k0_mm, 1)
            keys0_low(0)
            for s in range(SC):
                ctx_stats(0, s)
            ctx_mean(0)
            queries0_low(0)
            for s in range(SC):
                ctx_normalise(0, s)
            dve.wait_ge(k1w_h, 1)
            dve.tensor_tensor(flat(WK1l), PT_flat[:, 0:C * D], flat(WK1h).bitcast(F32), ALU.subtract)\
                .then_inc(k1w_l, 1)
            dve.wait_ge(pool_zero, 3)
            dve.wait_ge(l_row, 16)
            values0(0, SCO[:, 2, :])
            dve.wait_ge(l_rp, 16)
            dve.tensor_copy(RP[:, :, :], SX[:, 0:2, :]).then_inc(rep_id, 1)

            def batch(b, first, more):
                dve.wait_ge(l_mk0, 16 * b + 16)
                for k in range(35):
                    if k < 32:
                        shift(b, k)
                    if k == 0 and not first:
                        probs_out(b - 1, NH - 3)
                    if 3 <= k and (k - 3) % 4 == 1:
                        probs_out(b, k - 3)
                    if k == 1 and not first:
                        repeat_sums(b - 1, 2)
                    if k in (0, 2, 4, 6):
                        c = k // 2
                        if c == 0:
                            dve.wait_ge(ct_l, b + 1)
                            dve.wait_ge(ct_l2, 2 * b + 2)
                        dve.wait_ge(at_mm, 4 * b + c + 1)
                        dve.tensor_scalar(AT[:, c, 0:SC * SP], PJ[:, c % 2, 0:SC * SP], G1[:, c:c + 1], B1[:, c:c + 1],
                                          ALU.mult, ALU.add).then_inc(at_ev, 1)
                    if k == 7 and not first:
                        unit_outputs(b - 1, 2)
                    if k == 16 and not first:
                        result(b - 1)
                    if k - 2 in K1_DONE:
                        m = K1_DONE.index(k - 2)
                        dve.wait_ge(k1_h, 4 * b + m + 1)
                        dve.tensor_tensor(K1HL[:, m % 3, 1, :], PJ[:, m % 2, 0:SW], K1HL[:, m % 3, 0, :].bitcast(F32),
                                          ALU.subtract).then_inc(k1_l, 1)
                    if k == 18:
                        repeat_sums(b, 0)
                    if k == 23:
                        unit_outputs(b, 0)
                    if more and k in (14, 18, 20):
                        ctx_stats(b + 1, (14, 18, 20).index(k))
                    if more and k == 24:
                        ctx_mean(b + 1)
                    if more and k in (28, 29, 30):
                        ctx_normalise(b + 1, k - 28)
                    if k == 33:
                        repeat_sums(b, 1)
                unit_outputs(b, 1)
                dve.wait_ge(out0_mm, b + 1)
                dve.wait_ge(xb, b + 1)
                dve.tensor_tensor(R0[0:T, :], PJ[0:T, 1, :], R0[0:T, :], ALU.add).then_inc(res, 1)
                dve.wait_ge(res, b + 1)
                dve.bn_stats(YST[0:T, :], R0[0:T, :]).then_inc(y_st, 1)
                dve.wait_ge(y_st, b + 1)
                dve.sem_inc(met_dve, 1)
                dve.bn_aggr(YMV[0:T, :], YST[0:T, :]).then_inc(y_mv, 1)
                dve.wait_ge(y_mv, b + 1)
                dve.scalar_tensor_tensor(out=Y[0:T, :], in0=R0[0:T, :], scalar=YMV[0:T, 0:1], in1=G0[0:T, :],
                                         op0=ALU.subtract, op1=ALU.mult).then_inc(y_n, 1)
                dve.wait_ge(y_n, b + 1)
                dve.wait_ge(y_rs, b + 1)
                dve.scalar_tensor_tensor(out=Y[0:T, :], in0=Y[0:T, :], scalar=YRS[0:T, 0:1], in1=B0[0:T, :],
                                         op0=ALU.mult, op1=ALU.add).then_inc(y_ok, 1)
                if more:
                    for c in range(2):
                        dve.wait_ge(th_free, 3 * b + c + 1)
                        split_ctx(b + 1, c)
                dve.wait_ge(q1_h, b + 1)
                dve.tensor_tensor(QHL[:, 1, :, :].rearrange("p m t -> p (m t)"), PJ[:, 0, 0:C * T],
                                  QHL[:, 0, :, :].bitcast(F32).rearrange("p m t -> p (m t)"), ALU.subtract)\
                    .then_inc(q1_l, 1)
                for j in (1, 3):
                    dve.wait_ge(rep_mm, 4 * b + j + 1)
                    dve.tensor_copy(Q1S[:, j, :, :].rearrange("p m t -> p (m t)"), REP_BANK[j]).then_inc(rep_dve, 1)
                dve.wait_ge(mk1_b, b + 1)
                for k in range(32, NH):
                    shift(b, k)
                    if k == 32 and more:
                        dve.wait_ge(v1_mm, 3 * b + 3)
                        split_ctx_high(b + 1)
                    if k >= 35 and (k - 3) % 4 == 1:
                        probs_out(b, k - 3)
                    if more and k == 38:
                        queries0_low(b + 1)
                    if more and k == 40:
                        keys0_low(b + 1)
                    if more and k == 46:
                        values0(b + 1)

            batch(0, True, True)
            with dve.Fori(1, NB - 1) as b:
                batch(b, False, True)
            batch(NB - 1, False, False)
            probs_out(NB - 1, NH - 3)
            repeat_sums(NB - 1, 2)
            unit_outputs(NB - 1, 2)
            result(NB - 1)

        @block.scalar
        def _(act):
            def keys0_high(q):
                act.wait_ge(k0_mm, q + 1)
                act.activation(KHL[:, 0, :], PJ[:, 1, 0:SW], ACT.Identity, bias=BK0[:, 0:1]).then_inc(k0_h, 1)

            def values0_copied(q, bank=PJ[:, 0, :]):
                act.wait_ge(v0_mm, q + 1)
                wait_from(act, v0_tr, q)
                act.activation(V0T[:, :], bank[:, 0:SC * SP], ACT.Copy).then_inc(v0_t, 1)

            def queries0_high(q):
                act.wait_ge(q0_mm, q + 1)
                wait_from(act, rep_mm, 4 * q)
                for g in range(GR):
                    act.activation(QHL[:, 0, g, :], PJ[:, 0, g * T:(g + 1) * T], ACT.Identity,
                                   bias=BQ0[:, g:g + 1]).then_inc(q0_h, 1)

            def exps(b, k):
                act.wait_ge(shifted, NH * b + k + 1)
                if k >= 3 or not isinstance(b, int) or b > 0:
                    act.wait_ge(pt_mm, NH * b + k - 2)
                act.activation(PR[0:T, k % 3, 0:S], SCO[0:T, k % 3, 0:S], ACT.Exp, bias=MN[0:T, k:k + 1],
                               scale=-1.0, accum_out=SM[0:T, k:k + 1]).then_inc(prob, 1)

            def probs_out(b, k):
                act.wait_ge(pt_mm, NH * b + k + 1)
                h = k // HALF
                if k == 0 and isinstance(b, int) and b == 0:
                    act.wait_ge(k1w_l, 1)
                if k == 8 and isinstance(b, int) and b == 0:
                    act.wait_ge(v1w_l, 1)
                if k % HALF == 0:
                    wait_from(act, pv, NHALF * b + h - 1)
                act.activation(PT[0:SP, h % 2, k % HALF, :], TP[0:SP, k % 2, 0:SC * T], ACT.Copy).then_inc(pt_act, 1)

            def unit_sums(b, u, width):
                act.wait_ge(sums_t, 3 * b + u + 1)
                src = OA[:, 2 * T:4 * T] if u < 2 else PJ[:, 0, 0:C * T]
                act.activation(RI[:, 0:width], src, ACT.Copy).then_inc(inv, 1)

            def values1(b, s, bank):
                act.wait_ge(v1_mm, 3 * b + s + 1)
                act.activation(V1[0:SP, s, :], bank, ACT.Copy).then_inc(v1_ev, 1)

            act.wait_ge(l_k0, 16)
            act.activation(flat(WK0h), V1_flat[:, 0:C * P], ACT.Copy).then_inc(k0w_h, 1)
            act.wait_ge(l_sm, 16)
            act.activation(BQ0, BQ0, ACT.Copy, scale=SCALE0).then_inc(w_q0b, 1)
            act.wait_ge(l_q1, 16)
            act.activation(WQ0[:, :, :], WQ0[:, :, :], ACT.Copy, scale=SCALE0).then_inc(w_q0, 1)
            act.wait_ge(l_v0, 16)
            act.activation(flat(WV0h), V1_flat[:, C * P:2 * C * P], ACT.Copy).then_inc(v0w_h, 1)
            act.wait_ge(w_q0b, 1)
            keys0_high(0)
            act.wait_ge(l_k1, 16)
            act.activation(flat(WK1h), PT_flat[:, 0:C * D], ACT.Copy).then_inc(k1w_h, 1)
            queries0_high(0)
            act.wait_ge(l_row, 16)
            act.activation(GT, GT, ACT.Tanh).then_inc(gate_t, 1)
            values0_copied(0, SCO[:, 2, :])
            act.wait_ge(l_v1, 16)
            act.activation(flat(WV1h), PT_flat[:, WV1_AT:WV1_AT + C * D], ACT.Copy).then_inc(v1w_h, 1)

            def batch(b, first, more):
                for k in range(35):
                    if k == 0 and not first:
                        exps(b - 1, NH - 1)
                    if 1 <= k <= 32:
                        exps(b, k - 1)
                    if k in (1, 2) and not first:
                        probs_out(b - 1, NH - 3 + k)
                    if k >= 3 and (k - 3) % 4 != 1:
                        probs_out(b, k - 3)
                    if k in (1, 3, 5, 7):
                        c = k // 2
                        act.wait_ge(at_ev, 4 * b + c + 1)
                        act.wait_ge(v0_mm, b + 1)
                        act.activation(TH[:, c, 0:SC * SP], AT[:, c, 0:SC * SP], ACT.Copy).then_inc(at_h, 1)
                    if k == 6 and not first:
                        unit_sums(b - 1, 2, C * T)
                    if k == 22:
                        unit_sums(b, 0, 2 * T)
                    if k - 1 in K1_DONE:
                        m = K1_DONE.index(k - 1)
                        act.wait_ge(k1_mm, 4 * b + m + 1)
                        if m == 3:
                            act.wait_ge(k1st[0], 32 * b + 32)
                        elif m == 0 and not first:
                            act.wait_ge(k1st[1], 32 * b)
                        act.activation(K1HL[:, m % 3, 0, :], PJ[:, m % 2, 0:SW], ACT.Copy).then_inc(k1_h, 1)
                unit_sums(b, 1, 2 * T)
                values1(b, 0, PJ[0:SP, 0, :])
                values1(b, 1, SCO[0:SP, 0, :])
                act.wait_ge(yt_mm, b + 1)
                act.activation(YT[:, :, :].rearrange("p c t -> p (c t)"), PJ[:, 1, 0:C * T], ACT.Copy)\
                    .then_inc(yt_ev, 1)
                act.wait_ge(q1_mm, b + 1)
                act.wait_ge(qst, 16 * b + 16)
                act.activation(QHL[:, 0, :, :].rearrange("p m t -> p (m t)"), PJ[:, 0, 0:C * T], ACT.Copy)\
                    .then_inc(q1_h, 1)
                for j in (0, 2):
                    act.wait_ge(rep_mm, 4 * b + j + 1)
                    act.activation(Q1S[:, j, :, :].rearrange("p m t -> p (m t)"), REP_BANK[j], ACT.Copy)\
                        .then_inc(rep_act, 1)
                values1(b, 2, SCO[0:SP, 1, :])
                for k in range(33, NH):
                    exps(b, k - 1)
                    if k >= 35 and (k - 3) % 4 != 1:
                        probs_out(b, k - 3)
                    if more and k == 37:
                        queries0_high(b + 1)
                    if more and k == 39:
                        keys0_high(b + 1)
                    if more and k == 44:
                        values0_copied(b + 1)

            batch(0, True, True)
            with act.Fori(1, NB - 1) as b:
                batch(b, False, True)
            batch(NB - 1, False, False)
            exps(NB - 1, NH - 1)
            for k in (NH - 2, NH - 1):
                probs_out(NB - 1, k)
            unit_sums(NB - 1, 2, C * T)

        @block.gpsimd
        def _(pool):
            def split_ctx_low(q):
                pool.wait_ge(ct_h2, q + 1)
                pool.tensor_tensor(TL[:, 2:4, :], AT[:, 2:4, :], TH[:, 2:4, :].bitcast(F32), ALU.subtract)\
                    .then_inc(ct_l, 1)

            def ctx_rstd(q):
                pool.wait_ge(c_mv, 3 * q + 3)
                pool.sem_inc(met_pool, 1)
                pool.tensor_scalar(CVE[0:SP, :], CMV[0:SP, :, 1], EPS1, None, ALU.add).then_inc(c_ve, 1)
                pool.wait_ge(c_ve, q + 1)
                pool.tensor_tensor(CRS[0:SP, :], CVE[0:SP, :], mhalf[0:SP, :], ALU.pow).then_inc(c_rs, 1)

            pool.memset(V0P[:, :, :, :], 0.0).then_inc(pool_zero, 1)
            pool.memset(mhalf[:, :], -0.5).then_inc(pool_zero, 1)
            split_ctx_low(0)
            pool.memset(PR[:, :, :], 0.0).then_inc(pool_zero, 1)
            pool.wait_ge(pool_zero, 3)
            ctx_rstd(0)
            pool.wait_ge(l_row, 16)
            pool.wait_ge(v1w_h, 1)
            pool.tensor_tensor(flat(WV1l), PT_flat[:, WV1_AT:WV1_AT + C * D], flat(WV1h).bitcast(F32), ALU.subtract)\
                .then_inc(v1w_l, 1)

            def batch(b, more):
                for c in range(C):
                    pool.wait_ge(at_h, 4 * b + c + 1)
                    pool.tensor_tensor(TL[:, c, 0:SC * SP], AT[:, c, 0:SC * SP], TH[:, c, 0:SC * SP].bitcast(F32),
                                       ALU.subtract).then_inc(at_l, 1)
                pool.wait_ge(l_mk1, 16 * b + 16)
                wait_from(pool, shifted, NH * b)
                pool.sem_inc(met_pool, 1)
                pool.tensor_scalar(MK1[0:T, :], MU[0:T, :], -1.0, BIG, ALU.add, ALU.mult).then_inc(mk1_a, 1)
                pool.wait_ge(mk1_a, b + 1)
                pool.sem_inc(met_pool, 1)
                pool.tensor_scalar(MK1[0:T, :], MK1[0:T, :], BIG, None, ALU.mult).then_inc(mk1_b, 1)
                if more:
                    ctx_rstd(b + 1)
                pool.wait_ge(l_xn, 16 * b + 16)
                pool.tensor_tensor(R0[0:T, :], R0[0:T, :], BO0[0:T, :], ALU.add).then_inc(xb, 1)
                pool.wait_ge(y_mv, b + 1)
                pool.sem_inc(met_pool, 1)
                pool.tensor_scalar(YVE[0:T, :], YMV[0:T, 1:2], EPS0, None, ALU.add).then_inc(y_ve, 1)
                pool.wait_ge(y_ve, b + 1)
                pool.tensor_tensor(YRS[0:T, :], YVE[0:T, :], mhalf[0:T, 0:1], ALU.pow).then_inc(y_rs, 1)
                if more:
                    split_ctx_low(b + 1)

            batch(0, True)
            with pool.Fori(1, NB - 1) as b:
                batch(b, True)
            batch(NB - 1, False)


def kernel(**inputs):
    import numpy as np
    import concourse.bacc as bacc
    from concourse.bass_utils import run_bass_kernel_spmd

    a = {k: np.asarray(v) for k, v in inputs.items()}
    D, C, KVH, HD, GR = 512, 4, 8, 16, 4

    def chunked(w):
        return w.reshape(C, 128, -1).transpose(1, 0, 2)

    wq0 = a["L0_xattn_Wq"].reshape(D, 2, 4, GR, HD).transpose(0, 3, 1, 4, 2).reshape(D, D)
    wk0 = a["L0_xattn_Wk"].reshape(D, 2, 4, HD).transpose(0, 1, 3, 2).reshape(D, KVH * HD)
    wo0 = a["L0_xattn_Wo"].reshape(2, 4, 2, 2, HD, D).transpose(1, 2, 4, 0, 3, 5).reshape(128, C, D)
    bq0 = a["L0_xattn_bq"].reshape(2, 4, GR, HD).transpose(0, 3, 1, 2).reshape(128, GR)
    bk0 = a["L0_xattn_bk"].reshape(2, 4, HD).transpose(0, 2, 1).reshape(128, 1)
    repeat = np.zeros((4, 32, 2, 4, 32), np.float32)
    for r in range(4):
        repeat[:, range(32), r // 2, r, range(32)] = 1.0
    repeat = repeat.reshape(128, 2, 128)
    x, c = a["x"], a["ctx_2048"]
    arrays = {
        "x_rows": x,
        "x_cols": x.transpose(0, 2, 1).reshape(x.shape[0], C, 128, x.shape[1]).transpose(0, 2, 1, 3),
        "ctx_rows": c,
        "ctx_cols": c.transpose(0, 2, 1).reshape(c.shape[0], C, 128, c.shape[1]).transpose(0, 2, 1, 3),
        "mask0": a["mask_Bx1xSxS2_ff0"][:, 0],
        "mask1": a["mask_BxS2_bf1"],
        "wq0": chunked(wq0), "wk0": chunked(wk0), "wv0": chunked(a["L0_xattn_Wv"]), "wo0": wo0,
        "wq1": chunked(a["L1_xattn_Wq"].T), "wk1": chunked(a["L1_xattn_Wk"].T),
        "wv1": chunked(a["L1_xattn_Wv"].T), "wo1": chunked(a["L1_xattn_Wo"].T),
        "columns": np.concatenate([bq0, bk0, a["L1_xattn_ln_gamma"].reshape(C, 128).T,
                                   a["L1_xattn_ln_beta"].reshape(C, 128).T], axis=1),
        "rows": np.concatenate([a["L0_xattn_bv"], a["L0_xattn_bo"], a["L0_xattn_gamma"], a["L0_xattn_beta"],
                                a["L1_xattn_gate"]]),
        "identity": np.eye(128, dtype=np.float32),
        "repeat": repeat,
    }
    arrays = {k: np.ascontiguousarray(v) for k, v in arrays.items()}
    nc = bacc.Bacc("TRN2", target_bir_lowering=False, num_devices=1)
    args = [nc.dram_tensor(k, v.shape, mybir.dt.from_np(v.dtype), kind="ExternalInput").ap() for k, v in arrays.items()]
    out = nc.dram_tensor("out", x.shape, mybir.dt.float32, kind="ExternalOutput").ap()
    two_layer_cross_attention(nc, *args, out)
    r = run_bass_kernel_spmd(nc, [arrays], core_ids=[0])
    return r.results[0]["out"]
```
